# Optimizing a Trainium2 kernel written in Bass

```python
import numpy as np
import jax
import jax.numpy as jnp

def _softmax(x, axis=-1):
    return jax.nn.softmax(x, axis=axis)

def _gelu(x):
    return jax.nn.gelu(x, approximate=True)

def _silu(x):
    return jax.nn.silu(x)

def _sigmoid(x):
    return jax.nn.sigmoid(x)

def _layernorm(x, axis=-1, eps=1e-05):
    m = jnp.mean(x, axis=axis, keepdims=True)
    v = jnp.var(x, axis=axis, keepdims=True)
    return (x - m) / jnp.sqrt(v + eps)

def _scatter_add(tgt, idx, src, axis=0):
    return tgt.at[idx].add(src)

def _segment_sum(src, seg, n):
    return jax.ops.segment_sum(src, seg, n)
kernel_name = 'mk_adj_resnorm_d2_adj_r2_dfb6c8'

def setup_inputs(seed: int=0):
    np.random.seed(seed)
    _w = jnp.asarray

    def _rec_inputs():
        import jax
        import jax.numpy as jnp
        _gk = jax.random.key(seed)
        x = -0.0001538 + 1 * jax.random.normal(jax.random.fold_in(_gk, 1), (128, 64, 384), jnp.float32)
        _a = jax.random.bernoulli(jax.random.fold_in(_gk, 2), 0.0625, (128, 64, 64))
        _a = jnp.logical_or(_a, jnp.swapaxes(_a, -1, -2))
        _a = jnp.logical_or(_a, jnp.eye(64, dtype=bool))
        _af = _a.astype(jnp.float32)
        _af = _af * jax.random.uniform(jax.random.fold_in(_gk, 3), (128, 64, 64), jnp.float32, 0.05, 5.06092)
        adj = _af
        return (x, adj)
    x, adj = _rec_inputs()

    def _L0_gnn_setup():
        import jax, jax.numpy as jnp
        import numpy as np
        D_MODEL = 384
        NHEADS = 8
        D_FF = 1536
        B, N = (8, 512)
        EPS = 1e-06

        def _rmsnorm(x, alpha, gamma):
            x = x * jax.lax.rsqrt(jnp.mean(x * x, axis=-1, keepdims=True) + EPS)
            return alpha * x + gamma
        key = jax.random.key(seed)
        ks = jax.random.split(key, 10)
        d, f = (D_MODEL, D_FF)
        s = 1.0 / np.sqrt(d)
        inp = {'x': jax.random.normal(ks[0], (B, N, d), dtype=jnp.float32), 'attn_bias': jax.random.normal(ks[1], (B, N, N), dtype=jnp.float32), 'wq': jax.random.normal(ks[2], (d, d), dtype=jnp.float32) * s, 'bq': jnp.zeros((d,), jnp.float32), 'wk': jax.random.normal(ks[3], (d, d), dtype=jnp.float32) * s, 'bk': jnp.zeros((d,), jnp.float32), 'wv': jax.random.normal(ks[4], (d, d), dtype=jnp.float32) * s, 'bv': jnp.zeros((d,), jnp.float32), 'wo': jax.random.normal(ks[5], (d, d), dtype=jnp.float32) * s, 'bo': jnp.zeros((d,), jnp.float32), 'w1': jax.random.normal(ks[6], (d, f), dtype=jnp.float32) * s, 'b1': jnp.zeros((f,), jnp.float32), 'w2': jax.random.normal(ks[7], (f, d), dtype=jnp.float32) * (1.0 / np.sqrt(f)), 'b2': jnp.zeros((d,), jnp.float32), 'alpha1': jnp.ones((d,), jnp.float32), 'gamma1': jnp.ones((d,), jnp.float32), 'alpha2': jnp.ones((d,), jnp.float32), 'gamma2': jnp.ones((d,), jnp.float32)}
        return inp
    _L0_gnn_all = _L0_gnn_setup()
    _L0_gnn_in = {k: v for k, v in _L0_gnn_all.items() if k in ('wq', 'bq', 'wk', 'bk', 'wv', 'bv', 'wo', 'bo', 'w1', 'b1', 'w2', 'b2', 'alpha1', 'gamma1', 'alpha2', 'gamma2')}
    del _L0_gnn_all

    def _L1_gnn_setup():
        import jax, jax.numpy as jnp
        import numpy as np
        LN_EPS = 1e-12

        def _digcn_forward(hidden_state, adjacency_matrix, Wl, bl, Ws, bs, Wr, br, ln_w, ln_b):
            B, S, D = hidden_state.shape
            temper = jnp.asarray(D, jnp.float32) ** 0.5
            i = jnp.arange(S)
            upper = (i[None, :] > i[:, None]).astype(hidden_state.dtype)
            lower = (i[None, :] < i[:, None]).astype(hidden_state.dtype)

            def layer(h, params):
                wl, b_l, ws, b_s, wr, b_r, g, beta = params
                u = jnp.einsum('bid,bjd->bij', h, h) / temper
                a = jax.nn.softmax(u, axis=-1)
                delta = a * adjacency_matrix
                attn = delta / (jnp.sum(delta, axis=-1, keepdims=True) + 1e-10)
                hl = h @ wl.T + b_l
                hs = h @ ws.T + b_s
                hr = h @ wr.T + b_r
                diag_a = jnp.diagonal(attn, axis1=1, axis2=2)
                ctx = jnp.einsum('bij,bjd->bid', attn * upper, hl) + diag_a[..., None] * hs + jnp.einsum('bij,bjd->bid', attn * lower, hr)
                mean = ctx.mean(-1, keepdims=True)
                var = ctx.var(-1, keepdims=True)
                o = (ctx - mean) / jnp.sqrt(var + LN_EPS) * g + beta
                return (jax.nn.relu(o), None)
            out, _ = jax.lax.scan(layer, hidden_state, (Wl, bl, Ws, bs, Wr, br, ln_w, ln_b))
            return out
        key = jax.random.key(seed)
        ks = jax.random.split(key, 6)
        B, S, D, L = (8, 512, 384, 2)
        scale = (1.0 / D) ** 0.5
        hidden_state = jax.random.normal(ks[0], (B, S, D), jnp.float32)
        adjacency_matrix = (jax.random.uniform(ks[1], (B, S, S)) < 0.05).astype(jnp.float32)
        Wl = jax.random.normal(ks[2], (L, D, D), jnp.float32) * scale
        Ws = jax.random.normal(ks[3], (L, D, D), jnp.float32) * scale
        Wr = jax.random.normal(ks[4], (L, D, D), jnp.float32) * scale
        bl = jnp.zeros((L, D), jnp.float32)
        bs = jnp.zeros((L, D), jnp.float32)
        br = jnp.zeros((L, D), jnp.float32)
        ln_w = jnp.ones((L, D), jnp.float32)
        ln_b = jnp.zeros((L, D), jnp.float32)
        return dict(hidden_state=hidden_state, adjacency_matrix=adjacency_matrix, Wl=Wl, bl=bl, Ws=Ws, bs=bs, Wr=Wr, br=br, ln_w=ln_w, ln_b=ln_b)
    _L1_gnn_all = _L1_gnn_setup()
    _L1_gnn_in = {k: v for k, v in _L1_gnn_all.items() if k in ('Wl', 'bl', 'Ws', 'bs', 'Wr', 'br', 'ln_w', 'ln_b')}
    del _L1_gnn_all
    return {'x': x, 'adj': adj, 'L0_gnn_wq': _L0_gnn_in['wq'], 'L0_gnn_bq': _L0_gnn_in['bq'], 'L0_gnn_wk': _L0_gnn_in['wk'], 'L0_gnn_bk': _L0_gnn_in['bk'], 'L0_gnn_wv': _L0_gnn_in['wv'], 'L0_gnn_bv': _L0_gnn_in['bv'], 'L0_gnn_wo': _L0_gnn_in['wo'], 'L0_gnn_bo': _L0_gnn_in['bo'], 'L0_gnn_w1': _L0_gnn_in['w1'], 'L0_gnn_b1': _L0_gnn_in['b1'], 'L0_gnn_w2': _L0_gnn_in['w2'], 'L0_gnn_b2': _L0_gnn_in['b2'], 'L0_gnn_alpha1': _L0_gnn_in['alpha1'], 'L0_gnn_gamma1': _L0_gnn_in['gamma1'], 'L0_gnn_alpha2': _L0_gnn_in['alpha2'], 'L0_gnn_gamma2': _L0_gnn_in['gamma2'], 'L1_gnn_Wl': _L1_gnn_in['Wl'], 'L1_gnn_bl': _L1_gnn_in['bl'], 'L1_gnn_Ws': _L1_gnn_in['Ws'], 'L1_gnn_bs': _L1_gnn_in['bs'], 'L1_gnn_Wr': _L1_gnn_in['Wr'], 'L1_gnn_br': _L1_gnn_in['br'], 'L1_gnn_ln_w': _L1_gnn_in['ln_w'], 'L1_gnn_ln_b': _L1_gnn_in['ln_b']}

def reference(x, adj, L0_gnn_wq, L0_gnn_bq, L0_gnn_wk, L0_gnn_bk, L0_gnn_wv, L0_gnn_bv, L0_gnn_wo, L0_gnn_bo, L0_gnn_w1, L0_gnn_b1, L0_gnn_w2, L0_gnn_b2, L0_gnn_alpha1, L0_gnn_gamma1, L0_gnn_alpha2, L0_gnn_gamma2, L1_gnn_Wl, L1_gnn_bl, L1_gnn_Ws, L1_gnn_bs, L1_gnn_Wr, L1_gnn_br, L1_gnn_ln_w, L1_gnn_ln_b):
    import jax
    import jax.numpy as jnp

    def _L0_gnn_ref(x, attn_bias, wq, bq, wk, bk, wv, bv, wo, bo, w1, b1, w2, b2, alpha1, gamma1, alpha2, gamma2):
        import jax, jax.numpy as jnp
        import numpy as np
        D_MODEL = 384
        NHEADS = 8
        D_FF = 1536
        B, N = (8, 512)
        EPS = 1e-06

        def _rmsnorm(x, alpha, gamma):
            x = x * jax.lax.rsqrt(jnp.mean(x * x, axis=-1, keepdims=True) + EPS)
            return alpha * x + gamma
        b, n, d = x.shape
        h = NHEADS
        dh = d // h
        scaling = dh ** (-0.5)

        def split_heads(t):
            return t.reshape(b, n, h, dh).transpose(0, 2, 1, 3)
        q = split_heads(x @ wq + bq)
        k = split_heads(x @ wk + bk)
        v = split_heads(x @ wv + bv)
        scores = jnp.einsum('bhqd,bhkd->bhqk', q, k) * scaling
        scores = scores + attn_bias[:, None, :, :]
        attn = jax.nn.softmax(scores, axis=-1)
        ctx = jnp.einsum('bhij,bhjd->bhid', attn, v)
        ctx = ctx.transpose(0, 2, 1, 3).reshape(b, n, d)
        attn_out = ctx @ wo + bo
        x = _rmsnorm(x + attn_out, alpha1, gamma1)
        ff = jax.nn.silu(x @ w1 + b1) @ w2 + b2
        x = _rmsnorm(x + ff, alpha2, gamma2)
        return x

    def _L1_gnn_ref(hidden_state, adjacency_matrix, Wl, bl, Ws, bs, Wr, br, ln_w, ln_b):
        import jax, jax.numpy as jnp
        import numpy as np
        LN_EPS = 1e-12

        def _digcn_forward(hidden_state, adjacency_matrix, Wl, bl, Ws, bs, Wr, br, ln_w, ln_b):
            B, S, D = hidden_state.shape
            temper = jnp.asarray(D, jnp.float32) ** 0.5
            i = jnp.arange(S)
            upper = (i[None, :] > i[:, None]).astype(hidden_state.dtype)
            lower = (i[None, :] < i[:, None]).astype(hidden_state.dtype)

            def layer(h, params):
                wl, b_l, ws, b_s, wr, b_r, g, beta = params
                u = jnp.einsum('bid,bjd->bij', h, h) / temper
                a = jax.nn.softmax(u, axis=-1)
                delta = a * adjacency_matrix
                attn = delta / (jnp.sum(delta, axis=-1, keepdims=True) + 1e-10)
                hl = h @ wl.T + b_l
                hs = h @ ws.T + b_s
                hr = h @ wr.T + b_r
                diag_a = jnp.diagonal(attn, axis1=1, axis2=2)
                ctx = jnp.einsum('bij,bjd->bid', attn * upper, hl) + diag_a[..., None] * hs + jnp.einsum('bij,bjd->bid', attn * lower, hr)
                mean = ctx.mean(-1, keepdims=True)
                var = ctx.var(-1, keepdims=True)
                o = (ctx - mean) / jnp.sqrt(var + LN_EPS) * g + beta
                return (jax.nn.relu(o), None)
            out, _ = jax.lax.scan(layer, hidden_state, (Wl, bl, Ws, bs, Wr, br, ln_w, ln_b))
            return out
        return _digcn_forward(hidden_state, adjacency_matrix, Wl, bl, Ws, bs, Wr, br, ln_w, ln_b)
    x = _layernorm(x + _L0_gnn_ref(x, adj, L0_gnn_wq, L0_gnn_bq, L0_gnn_wk, L0_gnn_bk, L0_gnn_wv, L0_gnn_bv, L0_gnn_wo, L0_gnn_bo, L0_gnn_w1, L0_gnn_b1, L0_gnn_w2, L0_gnn_b2, L0_gnn_alpha1, L0_gnn_gamma1, L0_gnn_alpha2, L0_gnn_gamma2), axis=-1)
    x = _layernorm(x + _L1_gnn_ref(x, adj, L1_gnn_Wl, L1_gnn_bl, L1_gnn_Ws, L1_gnn_bs, L1_gnn_Wr, L1_gnn_br, L1_gnn_ln_w, L1_gnn_ln_b), axis=-1)
    return x

_drawn_inputs = setup_inputs


def setup_inputs(seed=0):
    import zlib

    import numpy as np

    out = dict(_drawn_inputs(seed))
    spreads = {'L0_gnn_bq': (0.0, 0.612),
     'L0_gnn_bk': (0.0, 2.0),
     'L0_gnn_bv': (0.0, 0.1),
     'L0_gnn_bo': (0.0, 0.1),
     'L0_gnn_b1': (0.0, 0.321),
     'L0_gnn_b2': (0.0, 0.1),
     'L0_gnn_alpha1': (1.0, 0.2),
     'L0_gnn_gamma1': (1.0, 0.2),
     'L0_gnn_alpha2': (1.0, 0.2),
     'L0_gnn_gamma2': (1.0, 0.2),
     'L1_gnn_bl': (0.0, 2.0),
     'L1_gnn_bs': (0.0, 0.1),
     'L1_gnn_br': (0.0, 2.0),
     'L1_gnn_ln_w': (1.0, 0.2),
     'L1_gnn_ln_b': (0.0, 0.1)}
    factors = {'L1_gnn_Wl': 3.417, 'L1_gnn_Wr': 3.625}
    for name, (base, spread) in spreads.items():
        noise = np.random.default_rng([zlib.crc32(name.encode()), seed]).standard_normal(out[name].shape)
        drawn = base * np.exp(spread * noise) if base else spread * noise
        out[name] = jnp.asarray(drawn.astype(out[name].dtype))
    for name, factor in factors.items():
        out[name] = (out[name] * factor).astype(out[name].dtype)
    return out
```

```python
from contextlib import ExitStack

import numpy as np

import concourse.bass as bass
from concourse import mybir

F32 = mybir.dt.float32
F32R = mybir.dt.float32r
ALU = mybir.AluOpType
ACT = mybir.ActivationFunctionType
AX_X = mybir.AxisListType.X

P = 128
GRAPHS, NODES, D = 128, 64, 384
TOKENS = GRAPHS * NODES
TILES = 2
STEP = TILES * P
STEPS = TOKENS // STEP
KC = D // P
HEADS = 8
DH = D // HEADS
FF = 1536
FC = FF // P
LAYERS = 2
QK_SCALE = float(DH) ** -0.5
U_SCALE = float(D) ** -0.5
RMS_EPS = 1e-6
NORM_EPS = 1e-5
CTX_EPS = 1e-12
FAR = -3.0e38

PIECES = [(h, c) for c in range(KC) for h in range(HEADS) if h * DH < (c + 1) * P and (h + 1) * DH > c * P]
NPIECE = len(PIECES)
HALF = P // 2
GAP = HALF - DH
CTX_FEATURE = np.array([[(2 * k + s) * DH + r if r < DH else (HEADS - 2 + s) * DH + GAP * k + r - DH
                         for s in range(2) for r in range(HALF)] for k in range(KC)])

WQ, WK, WV, WO, W1, W2 = 0, KC, 2 * KC, 3 * KC, 4 * KC, 4 * KC + KC * FF // D
WROWS = W2 + FC
C_MASK, C_BQ, C_BK, C_BV, C_B1 = 0, NPIECE, 2 * NPIECE, 2 * NPIECE + KC, 2 * NPIECE + 2 * KC
C_COLS = C_B1 + FC
R_BO, R_A1, R_G1, R_B2, R_A2, R_G2 = range(6)


class Signal:

    def __init__(self, sem, per_step=1, unit=1):
        self.sem, self.per_step, self.unit, self.whole = sem, per_step, unit, per_step * unit

    def upto(self, step, k=None):
        k = self.per_step - 1 if k is None else k
        value = (step * self.per_step + (self.per_step + k + 1)) * self.unit
        return max(value, 1) if isinstance(value, int) else value


def latest(j):
    return min(j + 1, STEPS - 1) if isinstance(j, int) else j + 1


def pipeline(eng, body):
    body(0, 0, None, None, 1)
    body(1, 1, 0, None, 2)
    with eng.Fori(2, STEPS - 1) as i:
        body(i, i, i - 1, i - 2, i + 1)
    body(STEPS - 1, STEPS - 1, STEPS - 2, STEPS - 3, None)
    body(STEPS, None, STEPS - 1, STEPS - 2, None)
    body(STEPS + 1, None, None, STEPS - 1, None)


def attention_block(nc, x, xT, adj, weights, cols, rows, ident, mid):
    ctx = ExitStack()
    with ctx:
        def sb(name, shape, dt=F32):
            return ctx.enter_context(nc.sbuf_tensor(name, shape, dt))

        def sig(name, per_step=1, unit=1):
            return Signal(ctx.enter_context(nc.semaphore("a_" + name)), per_step, unit)

        def sem(name):
            return ctx.enter_context(nc.semaphore("a_" + name))

        w_hi = sb("w_hi", [P, WROWS, D], F32R)
        w_lo = sb("w_lo", [P, WROWS, D], F32R)
        w1_hi = w_hi[:, W1:W2, :].rearrange("p (k c) d -> p k (c d)", k=KC)
        w1_lo = w_lo[:, W1:W2, :].rearrange("p (k c) d -> p k (c d)", k=KC)
        col = sb("col", [P, C_COLS])
        row = sb("row", [P, 6, D])
        idn = sb("idn", [P, P])
        half_power = sb("half_power", [P, TILES])
        x_in = sb("x_in", [P, TILES, D])
        xT_in = sb("xT_in", [P, KC, STEP])
        xT_hi = sb("xT_hi", [P, KC, STEP], F32R)
        xT_lo = sb("xT_lo", [P, KC, STEP], F32R)
        bias = sb("bias", [P, TILES, P])
        q_piece = sb("q_piece", [P, NPIECE, STEP])
        kT = sb("kT", [P, KC, STEP])
        v = sb("v", [P, TILES, D])
        prob = sb("prob", [P, TILES, HEADS, P])
        peak = sb("peak", [P, TILES, HEADS])
        shift = sb("shift", [P, TILES, HEADS])
        total = sb("total", [P, TILES, HEADS])
        share = sb("share", [P, TILES, HEADS])
        probT = sb("probT", [P, HEADS, P])
        headsT = sb("headsT", [P, HEADS // 2, STEP])
        ctxT_hi = sb("ctxT_hi", [P, KC, STEP], F32R)
        ctxT_lo = sb("ctxT_lo", [P, KC, STEP], F32R)
        res1 = sb("res1", [P, TILES, D])
        res2 = sb("res2", [P, TILES, D])
        x_gamma = sb("x_gamma", [P, TILES, D])
        squares = sb("squares", [P, TILES, D])
        power1 = sb("power1", [P, TILES])
        scale1 = sb("scale1", [P, TILES])
        power2 = sb("power2", [P, TILES])
        scale2 = sb("scale2", [P, TILES])
        stats = sb("stats", [P, TILES, 6])
        moments = sb("moments", [P, TILES, 2])
        rstd = sb("rstd", [P, TILES])
        offset = sb("offset", [P, TILES])
        normed = sb("normed", [P, TILES, D])
        x1T_hi = sb("x1T_hi", [P, KC, STEP], F32R)
        x1T_lo = sb("x1T_lo", [P, KC, STEP], F32R)
        tanh = sb("tanh", [P, 2, STEP])
        half = sb("half", [P, 2, STEP])
        gate = sb("gate", [P, 2, STEP])
        h_hi = sb("h_hi", [P, 3, STEP], F32R)
        h_lo = sb("h_lo", [P, 3, STEP], F32R)

        work = ctx.enter_context(nc.psum_tensor("work", [P, 4, 512], F32))
        hidden = ctx.enter_context(nc.psum_tensor("hidden", [P, 2, 512], F32))
        y = ctx.enter_context(nc.psum_tensor("y", [P, 2, 512], F32))

        def low(k, n):
            return work[:, k:k + (n + 511) // 512, :].rearrange("p b n -> p (b n)")[:, 0:n]

        stage = prob[:, :, :, :].rearrange("p t h n -> p t (h n)")

        piece_in = [sem("piece_in0"), sem("piece_in1")]
        const_in, consts = sem("const_in"), sem("consts")
        w_rounded, w_left = sem("w_rounded"), sem("w_left")
        passed_dve, passed_pool = sem("passed_dve"), sem("passed_pool")
        x_loaded = sig("x_loaded", 1, 16)
        xT_loaded = sig("xT_loaded", 1, 16)
        bias_loaded = sig("bias_loaded", 2, 16)
        ctx_moved = sig("ctx_moved", 2 * KC, 16)
        stored = sig("stored", 1, 16)
        xT_rounded = sig("xT_rounded")
        xT_left = sig("xT_left")
        q_ready = sig("q_ready", KC)
        k_ready = sig("k_ready", KC)
        v_ready = sig("v_ready", TILES)
        q_act = sig("q_act", 2)
        q_dve = sig("q_dve", 1)
        k_copied = sig("k_copied", KC)
        v_copied = sig("v_copied", TILES)
        s_ready = sig("s_ready", TILES)
        s_biased = sig("s_biased", 2 * TILES)
        s_peak = sig("s_peak", 2 * TILES)
        s_shift = sig("s_shift", TILES)
        s_exp = sig("s_exp", TILES)
        s_share = sig("s_share", TILES)
        p_scaled = sig("p_scaled", TILES)
        pT_ready = sig("pT_ready", TILES)
        pT_act = sig("pT_act", TILES)
        pT_dve = sig("pT_dve", TILES)
        c_ready = sig("c_ready", TILES)
        c_act = sig("c_act", TILES)
        c_dve = sig("c_dve", TILES)
        c_rounded = sig("c_rounded", KC)
        c_left = sig("c_left", KC)
        o_ready = sig("o_ready", TILES)
        o_added = sig("o_added", TILES)
        sq1 = sig("sq1", TILES)
        mean1 = sig("mean1", TILES)
        rms1 = sig("rms1", TILES)
        x1_scaled = sig("x1_scaled", TILES)
        x1_done = sig("x1_done", TILES)
        x1T_ready = sig("x1T_ready")
        x1T_rounded = sig("x1T_rounded")
        x1T_left = sig("x1T_left")
        h_ready = sig("h_ready", FC)
        h_tanh = sig("h_tanh", FC)
        h_half = sig("h_half", FC)
        h_gate = sig("h_gate", FC)
        h_rounded = sig("h_rounded", FC)
        h_left = sig("h_left", FC)
        y_added = sig("y_added", TILES)
        h_used = sig("h_used", FC)
        sq2 = sig("sq2", TILES)
        mean2 = sig("mean2", TILES)
        rms2 = sig("rms2", TILES)
        z_scaled = sig("z_scaled", TILES)
        z_done = sig("z_done", TILES)
        z_stats = sig("z_stats", TILES)
        z_moments = sig("z_moments", TILES)
        z_var = sig("z_var")
        z_rstd = sig("z_rstd")
        z_prod = sig("z_prod")
        z_offset = sig("z_offset")
        z_normed = sig("z_normed", TILES)
        res2_started = sig("res2_started")
        x_gamma_done = sig("x_gamma_done")
        res1_started = sig("res1_started")

        block = ctx.enter_context(nc.Block())

        @block.sync
        def _(sp):
            for s in (x_loaded, xT_loaded, bias_loaded, ctx_moved, stored):
                sp.sem_inc(s.sem, s.whole)
            sp.dma_start(col[:, :], cols).then_inc(const_in, 16)
            sp.dma_start(row[:, :, :], rows).then_inc(const_in, 16)
            sp.dma_start(idn[:, :], ident).then_inc(const_in, 16)

            def load_xT(n):
                sp.wait_ge(xT_left.sem, xT_left.upto(n - 1))
                sp.wait_ge(consts, 2)
                sp.dma_start(xT_in[:, :, :], xT.rearrange("(k p) n -> p k n", p=P)[:, :, bass.ts(n, STEP)])\
                    .then_inc(xT_loaded.sem, 16)

            def load_bias(a):
                sp.wait_ge(s_biased.sem, s_biased.upto(a - 1))
                sp.wait_ge(consts, 2)
                for g in range(2):
                    lanes = slice(g * NODES, (g + 1) * NODES)
                    sp.dma_start(bias[lanes, :, lanes],
                                 adj.rearrange("(s t p) n -> s p t n", t=TILES, p=P)[a, lanes])\
                        .then_inc(bias_loaded.sem, 16)

            for n in range(WROWS // 2):
                if n >= 2:
                    sp.wait_ge(w_left, n - 1)
                sp.dma_start(stage[:, n % 2, 0:2 * D], weights[:, n * 2 * D:(n + 1) * 2 * D])\
                    .then_inc(piece_in[n % 2], 16)
            sp.wait_ge(consts, 2)
            load_xT(0)

            def body(i, a, f, e, n):
                if a is not None:
                    load_bias(a)
                if n is not None:
                    load_xT(n)
                if a is not None:
                    sp.wait_ge(x_gamma_done.sem, x_gamma_done.upto(a - 1))
                    sp.wait_ge(consts, 2)
                    sp.dma_start(x_in[:, :, :], x.rearrange("(s t p) d -> s p t d", t=TILES, p=P)[a])\
                        .then_inc(x_loaded.sem, 16)
                if e is not None:
                    sp.wait_ge(z_normed.sem, z_normed.upto(e))
                    sp.wait_ge(consts, 2)
                    sp.dma_start(mid.rearrange("(s t p) d -> s p t d", t=TILES, p=P)[e], normed[:, :, :])\
                        .then_inc(stored.sem, 16)
                if a is not None:
                    sp.wait_ge(c_act.sem, c_act.upto(a))
                    sp.wait_ge(c_dve.sem, c_dve.upto(a))
                    for top in (0, HALF):
                        for k in range(KC):
                            sp.dma_start(headsT[top + DH:top + HALF, k, :],
                                         headsT[top + GAP * k:top + GAP * (k + 1), KC, :]).then_inc(ctx_moved.sem, 16)

            pipeline(sp, body)
            sp.wait_ge(stored.sem, stored.upto(STEPS - 1))

        @block.tensor
        def _(pe):
            for s in (q_ready, k_ready, v_ready, s_ready, pT_ready, c_ready, o_ready, x1T_ready,
                      h_ready, h_used):
                pe.sem_inc(s.sem, s.whole)
            pe.wait_ge(w_left, WROWS // 2)
            pe.wait_ge(const_in, 48)

            def product(out, left, right, ks):
                terms = [(k, u, w) for k in ks for u, w in ((0, 0), (0, 1), (1, 0))]
                for n, (k, u, w) in enumerate(terms):
                    mm = pe.matmul(out, left[u](k), right[w](k), start=(n == 0), stop=(n == len(terms) - 1))
                return mm

            def rows_of(w, r):
                return (lambda k: w_hi[:, r + k, :], lambda k: w_lo[:, r + k, :])

            def qk_chunk(a, w, m, bank):
                return product(low(bank, STEP),
                               (lambda k: w_hi[:, w + k, m * P:(m + 1) * P], lambda k: w_lo[:, w + k, m * P:(m + 1) * P]),
                               (lambda k: xT_hi[:, k, :], lambda k: xT_lo[:, k, :]), range(KC))

            def queries_keys(a):
                pe.wait_ge(xT_left.sem, xT_left.upto(a))
                pe.wait_ge(pT_act.sem, pT_act.upto(a - 1))
                pe.wait_ge(pT_dve.sem, pT_dve.upto(a - 1))
                for m in range(KC):
                    if m == 2:
                        pe.wait_ge(c_act.sem, c_act.upto(a - 1))
                        pe.wait_ge(c_dve.sem, c_dve.upto(a - 1))
                    qk_chunk(a, WQ, m, m).then_inc(q_ready.sem, 1)
                for m in range(KC):
                    if m:
                        prior = q_act if m == 1 else q_dve
                        pe.wait_ge(prior.sem, prior.upto(a, 0))
                    qk_chunk(a, WK, m, (3 + m) % 4).then_inc(k_ready.sem, 1)

            def transpose_x1(f, a):
                if a is not None:
                    pe.wait_ge(v_copied.sem, v_copied.upto(a))
                for t in range(TILES):
                    pe.wait_ge(x1_done.sem, x1_done.upto(f, t))
                    for k in range(KC):
                        mm = pe.transpose(low(0, KC * STEP)[:, k * STEP + t * P:k * STEP + (t + 1) * P],
                                          res1[:, t, k * P:(k + 1) * P], idn[:, :])
                mm.then_inc(x1T_ready.sem, 1)

            def token_major(out, left_hi, left_lo, t, w):
                return product(out, (lambda k: left_hi[:, k, t * P:(t + 1) * P], lambda k: left_lo[:, k, t * P:(t + 1) * P]),
                               rows_of(None, w), range(KC))

            def values(a):
                for t in range(TILES):
                    pe.wait_ge(k_copied.sem, k_copied.upto(a, t + 1))
                    token_major(low(t, D), xT_hi, xT_lo, t, WV).then_inc(v_ready.sem, 1)

            def scores(a, f, t):
                if t == 0 and f is not None:
                    pe.wait_ge(o_added.sem, o_added.upto(f))
                elif t == 0:
                    pe.wait_ge(k_copied.sem, k_copied.upto(a, 0))
                pe.wait_ge(k_copied.sem, k_copied.upto(a))
                pe.wait_ge(q_act.sem, q_act.upto(a))
                pe.wait_ge(q_dve.sem, q_dve.upto(a))
                s = low(2, HEADS * P)
                for h in range(HEADS):
                    if t == 1 and h % 4 == 0:
                        pe.wait_ge(s_biased.sem, s_biased.upto(a, h // 4))
                    own = [j for j, (head, _) in enumerate(PIECES) if head == h]
                    for j in own:
                        mm = pe.matmul(s[:, h * P:(h + 1) * P], q_piece[:, j, t * P:(t + 1) * P],
                                       kT[:, PIECES[j][1], t * P:(t + 1) * P], start=(j == own[0]), stop=(j == own[-1]))
                mm.then_inc(s_ready.sem, 1)

            def transpose_probs(a, f, t):
                pe.wait_ge(p_scaled.sem, p_scaled.upto(a, t))
                if t == 1:
                    pe.wait_ge(pT_act.sem, pT_act.upto(a, 0))
                    pe.wait_ge(pT_dve.sem, pT_dve.upto(a, 0))
                elif f is not None:
                    pe.wait_ge(x1T_left.sem, x1T_left.upto(f))
                else:
                    pe.wait_ge(v_copied.sem, v_copied.upto(a))
                for h in range(HEADS):
                    mm = pe.transpose(low(0, HEADS * P)[:, h * P:(h + 1) * P], prob[:, t, h, :], idn[:, :])
                mm.then_inc(pT_ready.sem, 1)

            def contexts(a, t):
                pe.wait_ge(pT_act.sem, pT_act.upto(a, t))
                pe.wait_ge(pT_dve.sem, pT_dve.upto(a, t))
                pe.wait_ge(v_copied.sem, v_copied.upto(a, t))
                pe.wait_ge(s_biased.sem, s_biased.upto(a))
                for h in range(HEADS):
                    base = 64 * (h % 2)
                    mm = pe.matmul(work[base:base + DH, 2 + t, (h // 2) * P:(h // 2 + 1) * P],
                                   v[:, t, h * DH:(h + 1) * DH], probT[:, h, :], start=True, stop=True)
                mm.then_inc(c_ready.sem, 1)

            def hidden_chunk(f, c):
                if c == 0:
                    pe.wait_ge(x1T_rounded.sem, x1T_rounded.upto(f))
                    pe.wait_ge(x1T_left.sem, x1T_left.upto(f))
                pe.wait_ge(h_tanh.sem, h_tanh.upto(f, c - 2))
                pe.wait_ge(h_half.sem, h_half.upto(f, c - 2))
                product(hidden[:, c % 2, 0:STEP],
                        (lambda k: w1_hi[:, k, c * P:(c + 1) * P], lambda k: w1_lo[:, k, c * P:(c + 1) * P]),
                        (lambda k: x1T_hi[:, k, :], lambda k: x1T_lo[:, k, :]), range(KC)).then_inc(h_ready.sem, 1)

            def down(f, c):
                pe.wait_ge(h_rounded.sem, h_rounded.upto(f, c))
                pe.wait_ge(h_left.sem, h_left.upto(f, c))
                if c == 0:
                    pe.wait_ge(y_added.sem, y_added.upto(f - 1))
                for t in range(TILES):
                    for n, (hh, ww) in enumerate(((h_hi, w_hi), (h_hi, w_lo), (h_lo, w_hi))):
                        mm = pe.matmul(y[:, t, 0:D], hh[:, c % 3, t * P:(t + 1) * P], ww[:, W2 + c, :],
                                       start=(c == 0 and n == 0), stop=(c == FC - 1 and n == 2))
                mm.then_inc(h_used.sem, 1)

            def output(a, keys_too):
                pe.wait_ge(c_rounded.sem, c_rounded.upto(a))
                pe.wait_ge(c_left.sem, c_left.upto(a))
                if keys_too:
                    pe.wait_ge(q_act.sem, q_act.upto(a + 1))
                    pe.wait_ge(k_copied.sem, k_copied.upto(a + 1, 0))
                for t in range(TILES):
                    token_major(low(2 + t, D), ctxT_hi, ctxT_lo, t, WO).then_inc(o_ready.sem, 1)

            def body(i, a, f, e, n):
                if a is not None:
                    queries_keys(a)
                if f is not None:
                    output(f, a is not None)
                if a is not None:
                    values(a)
                    scores(a, f, 0)
                if f is not None:
                    transpose_x1(f, a)
                if a is not None:
                    scores(a, f, 1)
                for c in range(FC):
                    if f is not None:
                        hidden_chunk(f, c)
                        if c >= 2:
                            down(f, c - 2)
                    if a is not None:
                        if c == 6:
                            transpose_probs(a, f, 0)
                        if c == 7:
                            contexts(a, 0)
                        if c == 10:
                            transpose_probs(a, f, 1)
                        if c == 11:
                            contexts(a, 1)
                if f is not None:
                    down(f, FC - 2)
                    down(f, FC - 1)

            pipeline(pe, body)

        @block.scalar
        def _(act):
            for s in (xT_rounded, q_act, s_exp, pT_act, c_act, c_rounded, sq1, x1T_rounded, h_tanh,
                      h_rounded, sq2, z_normed):
                act.sem_inc(s.sem, s.whole)
            act.wait_ge(const_in, 48)
            act.wait_ge(consts, 4)

            def round_xT(n):
                act.wait_ge(xT_loaded.sem, xT_loaded.upto(n))
                act.wait_ge(v_ready.sem, v_ready.upto(n - 1))
                act.activation(xT_hi[:, :, :], xT_in[:, :, :], ACT.Copy).then_inc(xT_rounded.sem, 1)

            def query_pieces(a, m):
                act.wait_ge(q_ready.sem, q_ready.upto(a, m))
                if m == 0:
                    act.wait_ge(s_ready.sem, s_ready.upto(a - 1))
                own = [j for j, (_, c) in enumerate(PIECES) if c == m]
                for j in own:
                    ins = act.activation(q_piece[:, j, :], low(m, STEP), ACT.Identity,
                                         bias=col[:, C_BQ + j:C_BQ + j + 1], scale=col[:, C_MASK + j:C_MASK + j + 1])
                ins.then_inc(q_act.sem, 1)

            def exps(a, t, heads):
                if heads[0] == 0:
                    act.wait_ge(s_shift.sem, s_shift.upto(a, t))
                for h in heads:
                    ins = act.activation(prob[:, t, h, :], prob[:, t, h, :], ACT.Exp,
                                         bias=shift[:, t, h:h + 1], accum_out=total[:, t, h:h + 1])
                if heads[-1] == HEADS - 1:
                    ins.then_inc(s_exp.sem, 1)

            def copy_probT(a, t):
                act.wait_ge(pT_ready.sem, pT_ready.upto(a, t))
                act.wait_ge(c_ready.sem, c_ready.upto(a - 1 if t == 0 else a, 1 - t))
                act.activation(probT[:, 0:4, :], work[:, 0, :].rearrange("p (h n) -> p h n", n=P), ACT.Copy)\
                    .then_inc(pT_act.sem, 1)

            def copy_heads(a, t):
                act.wait_ge(c_ready.sem, c_ready.upto(a, t))
                act.wait_ge(c_rounded.sem, c_rounded.upto(a - 1))
                act.wait_ge(c_left.sem, c_left.upto(a - 1))
                act.activation(headsT[0:DH, :, t * P:(t + 1) * P],
                               work[0:DH, 2 + t, :].rearrange("p (h n) -> p h n", n=P), ACT.Copy).then_inc(c_act.sem, 1)

            def round_ctx(a):
                act.wait_ge(ctx_moved.sem, ctx_moved.upto(a))
                act.wait_ge(o_ready.sem, o_ready.upto(a - 1))
                for k in range(KC):
                    act.activation(ctxT_hi[:, k, :], headsT[:, k, :], ACT.Identity, bias=col[:, C_BV + k:C_BV + k + 1])\
                        .then_inc(c_rounded.sem, 1)

            def square_sums(added, t, f, buf, power, done, other, last):
                act.wait_ge(added.sem, added.upto(f, t))
                act.wait_ge(other.sem, other.upto(last, t))
                act.activation(squares[:, t, :], buf[:, t, :], ACT.Square, accum_out=power[:, t:t + 1])\
                    .then_inc(done.sem, 1)

            def round_x1T(f):
                act.wait_ge(x1T_ready.sem, x1T_ready.upto(f))
                act.wait_ge(h_ready.sem, h_ready.upto(f - 1))
                act.activation(x1T_hi[:, :, :].rearrange("p k n -> p (k n)"), low(0, KC * STEP), ACT.Copy)\
                    .then_inc(x1T_rounded.sem, 1)

            def tanh_chunk(f, c):
                act.wait_ge(h_ready.sem, h_ready.upto(f, c))
                act.wait_ge(h_gate.sem, h_gate.upto(f, c - 2))
                act.activation(tanh[:, c % 2, :], hidden[:, c % 2, 0:STEP], ACT.Tanh,
                               bias=col[:, C_B1 + c:C_B1 + c + 1], scale=0.5).then_inc(h_tanh.sem, 1)

            def round_chunk(f, c):
                act.wait_ge(h_gate.sem, h_gate.upto(f, c))
                act.wait_ge(h_used.sem, h_used.upto(f, c - 3))
                act.activation(h_hi[:, c % 3, :], gate[:, c % 2, :], ACT.Copy).then_inc(h_rounded.sem, 1)

            def norm_out(e):
                act.wait_ge(z_offset.sem, z_offset.upto(e))
                act.wait_ge(stored.sem, stored.upto(e - 1))
                for t in range(TILES):
                    act.activation(normed[:, t, :], res2[:, t, :], ACT.Identity, bias=offset[:, t:t + 1],
                                   scale=rstd[:, t:t + 1]).then_inc(z_normed.sem, 1)

            round_xT(0)

            def body(i, a, f, e, n):
                if a is not None:
                    query_pieces(a, 0)
                if f is not None:
                    round_ctx(f)
                if a is not None:
                    query_pieces(a, 2)
                if f is not None:
                    for t in range(TILES):
                        square_sums(o_added, t, f, res1, power1, sq1, sq2, f - 1)
                    round_x1T(f)
                for c in range(FC):
                    if f is not None:
                        tanh_chunk(f, c)
                        if c:
                            round_chunk(f, c - 1)
                    if a is not None:
                        if c < 8:
                            exps(a, c // 4, range(2 * (c % 4), 2 * (c % 4) + 2))
                        if c == 6:
                            copy_probT(a, 0)
                        if c == 7:
                            copy_heads(a, 0)
                        if c == 10:
                            copy_probT(a, 1)
                    if e is not None and c == 8:
                        norm_out(e)
                    if n is not None and c == 9:
                        round_xT(n)
                if f is not None:
                    round_chunk(f, FC - 1)
                if a is not None:
                    copy_heads(a, 1)
                if f is not None:
                    for t in range(TILES):
                        square_sums(y_added, t, f, res2, power2, sq2, sq1, f)

            pipeline(act, body)

        @block.vector
        def _(dve):
            for s in (xT_left, q_dve, k_copied, v_copied, s_biased, s_peak, s_shift, s_share, pT_dve,
                      c_dve, c_left, o_added, x1_scaled, x1T_left, h_half, h_gate, y_added, z_scaled,
                      z_done, z_stats, z_moments):
                dve.sem_inc(s.sem, s.whole)
            dve.memset(bias[:, :, :], FAR).then_inc(consts, 1)
            dve.memset(half_power[:, :], -0.5).then_inc(consts, 1)
            dve.wait_ge(const_in, 48)
            dve.tensor_tensor(col[:, C_BQ:C_BQ + NPIECE], col[:, C_BQ:C_BQ + NPIECE], col[:, C_MASK:C_MASK + NPIECE],
                              ALU.mult).then_inc(consts, 1)
            dve.tensor_scalar(col[:, C_B1:C_B1 + FC], col[:, C_B1:C_B1 + FC], 0.5, None, ALU.mult)\
                .then_inc(consts, 1)
            for n in range(WROWS // 2):
                src = stage[:, n % 2, 0:2 * D].rearrange("p (r d) -> p r d", d=D)
                rows_ = slice(2 * n, 2 * n + 2)
                dve.wait_ge(piece_in[n % 2], 16 * (n // 2 + 1))
                dve.tensor_copy(w_hi[:, rows_, :], src).then_inc(w_rounded, 1)
                dve.wait_ge(w_rounded, n + 1)
                dve.tensor_tensor(w_lo[:, rows_, :], src, w_hi[:, rows_, :].bitcast(F32), ALU.subtract)\
                    .then_inc(w_left, 1)
            dve.wait_ge(consts, 4)

            def left_xT(n):
                dve.wait_ge(xT_rounded.sem, xT_rounded.upto(n))
                dve.wait_ge(v_ready.sem, v_ready.upto(n - 1))
                dve.tensor_tensor(xT_lo[:, :, :], xT_in[:, :, :], xT_hi[:, :, :].bitcast(F32), ALU.subtract)\
                    .then_inc(xT_left.sem, 1)

            def query_pieces(a, m):
                dve.wait_ge(q_ready.sem, q_ready.upto(a, m))
                dve.wait_ge(s_ready.sem, s_ready.upto(a - 1))
                own = [j for j, (_, c) in enumerate(PIECES) if c == m]
                for j in own:
                    ins = dve.tensor_scalar(q_piece[:, j, :], low(m, STEP), col[:, C_MASK + j:C_MASK + j + 1],
                                            col[:, C_BQ + j:C_BQ + j + 1], ALU.mult, ALU.add)
                ins.then_inc(q_dve.sem, 1)

            def keys(a, m):
                dve.wait_ge(k_ready.sem, k_ready.upto(a, m))
                if m == 0:
                    dve.wait_ge(s_ready.sem, s_ready.upto(a - 1))
                dve.tensor_scalar(kT[:, m, :], low((3 + m) % 4, STEP), col[:, C_BK + m:C_BK + m + 1], None, ALU.add)\
                    .then_inc(k_copied.sem, 1)

            def copy_values(a, t):
                dve.wait_ge(v_ready.sem, v_ready.upto(a, t))
                dve.wait_ge(c_ready.sem, c_ready.upto(a - 1, t))
                dve.tensor_copy(v[:, t, :], low(t, D)).then_inc(v_copied.sem, 1)

            def bias_scores(a, t):
                dve.wait_ge(s_ready.sem, s_ready.upto(a, t))
                dve.wait_ge(bias_loaded.sem, bias_loaded.upto(a))
                dve.wait_ge(pT_ready.sem, pT_ready.upto(a - 1, t))
                for g in range(2):
                    heads = slice(4 * g, 4 * g + 4)
                    dve.scalar_tensor_tensor(out=prob[:, t, heads, :], in0=work[:, 2 + g, :].rearrange("p (h n) -> p h n", n=P),
                                             scalar=QK_SCALE, in1=bias[:, t, None, :].broadcast_to([P, 4, P]),
                                             op0=ALU.mult, op1=ALU.add).then_inc(s_biased.sem, 1)

            def softmax_peak(a, t, g):
                dve.wait_ge(s_biased.sem, s_biased.upto(a, 2 * t + g))
                heads = slice(4 * g, 4 * g + 4)
                dve.tensor_reduce(peak[:, t, heads], prob[:, t, heads, :], AX_X, ALU.max).then_inc(s_peak.sem, 1)
                if g == 1:
                    dve.wait_ge(s_peak.sem, s_peak.upto(a, 2 * t + 1))
                    dve.tensor_scalar(shift[:, t, :], peak[:, t, :], -1.0, None, ALU.mult).then_inc(s_shift.sem, 1)

            def softmax_share(a, t):
                dve.wait_ge(s_exp.sem, s_exp.upto(a, t))
                dve.reciprocal(share[:, t, :], total[:, t, :]).then_inc(s_share.sem, 1)

            def copy_probT(a, t):
                dve.wait_ge(pT_ready.sem, pT_ready.upto(a, t))
                dve.wait_ge(c_ready.sem, c_ready.upto(a - 1 if t == 0 else a, 1 - t))
                dve.tensor_copy(probT[:, 4:8, :], work[:, 1, :].rearrange("p (h n) -> p h n", n=P))\
                    .then_inc(pT_dve.sem, 1)

            def copy_heads(a, t):
                dve.wait_ge(c_ready.sem, c_ready.upto(a, t))
                dve.wait_ge(c_left.sem, c_left.upto(a - 1))
                dve.tensor_copy(headsT[64:64 + DH, :, t * P:(t + 1) * P],
                                work[64:64 + DH, 2 + t, :].rearrange("p (h n) -> p h n", n=P)).then_inc(c_dve.sem, 1)

            def left_ctx(a):
                dve.wait_ge(o_ready.sem, o_ready.upto(a - 1))
                for k in range(KC):
                    dve.wait_ge(c_rounded.sem, c_rounded.upto(a, k))
                    dve.scalar_tensor_tensor(out=ctxT_lo[:, k, :], in0=headsT[:, k, :], scalar=col[:, C_BV + k:C_BV + k + 1],
                                             in1=ctxT_hi[:, k, :].bitcast(F32), op0=ALU.add, op1=ALU.subtract)\
                        .then_inc(c_left.sem, 1)

            def add_output(f, t):
                dve.wait_ge(o_ready.sem, o_ready.upto(f, t))
                dve.wait_ge(res1_started.sem, res1_started.upto(f))
                dve.tensor_tensor(res1[:, t, :], low(2 + t, D), res1[:, t, :], ALU.add).then_inc(o_added.sem, 1)

            def scale_x1(f, t):
                dve.wait_ge(rms1.sem, rms1.upto(f, t))
                dve.scalar_tensor_tensor(out=res1[:, t, :], in0=res1[:, t, :], scalar=scale1[:, t:t + 1],
                                         in1=row[:, R_A1, :], op0=ALU.mult, op1=ALU.mult).then_inc(x1_scaled.sem, 1)

            def left_x1T(f):
                dve.wait_ge(x1T_rounded.sem, x1T_rounded.upto(f))
                dve.wait_ge(h_ready.sem, h_ready.upto(f - 1))
                dve.tensor_tensor(x1T_lo[:, :, :].rearrange("p k n -> p (k n)"), low(0, KC * STEP),
                                  x1T_hi[:, :, :].rearrange("p k n -> p (k n)").bitcast(F32), ALU.subtract)\
                    .then_inc(x1T_left.sem, 1)

            def gate_chunk(f, c):
                dve.wait_ge(h_tanh.sem, h_tanh.upto(f, c))
                dve.tensor_scalar(half[:, c % 2, :], hidden[:, c % 2, 0:STEP], 0.5, col[:, C_B1 + c:C_B1 + c + 1],
                                  ALU.mult, ALU.add).then_inc(h_half.sem, 1)
                dve.wait_ge(h_half.sem, h_half.upto(f, c))
                dve.wait_ge(h_rounded.sem, h_rounded.upto(f, c - 2))
                dve.wait_ge(h_left.sem, h_left.upto(f, c - 2))
                dve.scalar_tensor_tensor(out=gate[:, c % 2, :], in0=tanh[:, c % 2, :], scalar=1.0,
                                         in1=half[:, c % 2, :], op0=ALU.add, op1=ALU.mult).then_inc(h_gate.sem, 1)

            def add_down(f, t):
                dve.wait_ge(h_used.sem, h_used.upto(f))
                dve.wait_ge(res2_started.sem, res2_started.upto(f))
                dve.tensor_tensor(res2[:, t, :], y[:, t, 0:D], res2[:, t, :], ALU.add).then_inc(y_added.sem, 1)

            def last_sum(e, t):
                dve.wait_ge(rms2.sem, rms2.upto(e, t))
                dve.scalar_tensor_tensor(out=res2[:, t, :], in0=res2[:, t, :], scalar=scale2[:, t:t + 1],
                                         in1=row[:, R_A2, :], op0=ALU.mult, op1=ALU.mult).then_inc(z_scaled.sem, 1)
                dve.wait_ge(z_scaled.sem, z_scaled.upto(e, t))
                dve.wait_ge(x_gamma_done.sem, x_gamma_done.upto(e))
                dve.tensor_tensor(res2[:, t, :], res2[:, t, :], x_gamma[:, t, :], ALU.add).then_inc(z_done.sem, 1)
                dve.wait_ge(z_done.sem, z_done.upto(e, t))
                dve.bn_stats(stats[:, t, :], res2[:, t, :]).then_inc(z_stats.sem, 1)
                dve.wait_ge(z_stats.sem, z_stats.upto(e, t))
                dve.sem_inc(passed_dve, 1)
                dve.bn_aggr(moments[:, t, :], stats[:, t, :]).then_inc(z_moments.sem, 1)

            left_xT(0)

            def body(i, a, f, e, n):
                if a is not None:
                    query_pieces(a, 1)
                    keys(a, 0)
                if f is not None:
                    left_ctx(f)
                if a is not None:
                    keys(a, 1)
                    keys(a, 2)
                if f is not None:
                    for t in range(TILES):
                        add_output(f, t)
                if a is not None:
                    copy_values(a, 0)
                if f is not None:
                    scale_x1(f, 0)
                if a is not None:
                    copy_values(a, 1)
                if f is not None:
                    scale_x1(f, 1)
                if a is not None:
                    bias_scores(a, 0)
                if f is not None:
                    left_x1T(f)
                if a is not None:
                    softmax_peak(a, 0, 0)
                    softmax_peak(a, 0, 1)
                for c in range(FC):
                    if f is not None:
                        gate_chunk(f, c)
                    if a is not None:
                        if c == 0:
                            bias_scores(a, 1)
                        if c == 1:
                            softmax_peak(a, 1, 0)
                        if c == 2:
                            softmax_peak(a, 1, 1)
                        if c == 4:
                            softmax_share(a, 0)
                        if c == 6:
                            copy_probT(a, 0)
                        if c == 7:
                            copy_heads(a, 0)
                        if c == 8:
                            softmax_share(a, 1)
                        if c == 10:
                            copy_probT(a, 1)
                    if e is not None and c in (3, 5):
                        last_sum(e, (c - 3) // 2)
                    if n is not None and c == 9:
                        left_xT(n)
                if a is not None:
                    copy_heads(a, 1)
                if f is not None:
                    for t in range(TILES):
                        add_down(f, t)

            pipeline(dve, body)

        @block.gpsimd
        def _(pool):
            for s in (p_scaled, mean1, rms1, x1_done, h_left, mean2, rms2, z_var, z_rstd, z_prod, z_offset,
                      res2_started, x_gamma_done, res1_started):
                pool.sem_inc(s.sem, s.whole)
            pool.wait_ge(const_in, 48)
            pool.wait_ge(consts, 2)

            def rms(f, t, done, power, scale, mean, ready):
                pool.wait_ge(done.sem, done.upto(f, t))
                pool.sem_inc(passed_pool, 1)
                pool.tensor_scalar(power[:, t:t + 1], power[:, t:t + 1], 1.0 / D, RMS_EPS, ALU.mult, ALU.add)\
                    .then_inc(mean.sem, 1)
                pool.wait_ge(mean.sem, mean.upto(f, t))
                pool.tensor_tensor(scale[:, t:t + 1], power[:, t:t + 1], half_power[:, 0:1], ALU.pow)\
                    .then_inc(ready.sem, 1)

            def finish_x1(f, t):
                pool.wait_ge(x1_scaled.sem, x1_scaled.upto(f, t))
                pool.tensor_tensor(res1[:, t, :], res1[:, t, :], row[:, R_G1, :], ALU.add).then_inc(x1_done.sem, 1)

            def last_norm(e):
                pool.wait_ge(z_moments.sem, z_moments.upto(e))
                pool.sem_inc(passed_pool, 1)
                pool.tensor_scalar(rstd[:, :], moments[:, :, 1], 1.0, NORM_EPS, ALU.mult, ALU.add)\
                    .then_inc(z_var.sem, 1)
                pool.wait_ge(z_var.sem, z_var.upto(e))
                pool.tensor_tensor(rstd[:, :], rstd[:, :], half_power[:, :], ALU.pow).then_inc(z_rstd.sem, 1)
                pool.wait_ge(z_rstd.sem, z_rstd.upto(e))
                pool.tensor_tensor(offset[:, :], moments[:, :, 0], rstd[:, :], ALU.mult).then_inc(z_prod.sem, 1)
                pool.wait_ge(z_prod.sem, z_prod.upto(e))
                pool.sem_inc(passed_pool, 1)
                pool.tensor_scalar(offset[:, :], offset[:, :], -1.0, None, ALU.mult).then_inc(z_offset.sem, 1)

            def start_res2(f):
                pool.wait_ge(x1_done.sem, x1_done.upto(f))
                pool.wait_ge(z_normed.sem, z_normed.upto(f - 1))
                pool.tensor_tensor(res2[:, :, :], res1[:, :, :], row[:, R_B2, None, :].broadcast_to([P, TILES, D]), ALU.add)\
                    .then_inc(res2_started.sem, 1)

            def add_gamma(f):
                pool.wait_ge(x_loaded.sem, x_loaded.upto(f))
                pool.wait_ge(z_done.sem, z_done.upto(f - 1))
                pool.tensor_tensor(x_gamma[:, :, :], x_in[:, :, :], row[:, R_G2, None, :].broadcast_to([P, TILES, D]), ALU.add)\
                    .then_inc(x_gamma_done.sem, 1)

            def start_res1(a):
                pool.wait_ge(x_loaded.sem, x_loaded.upto(a))
                pool.wait_ge(x1T_ready.sem, x1T_ready.upto(a - 1))
                pool.wait_ge(res2_started.sem, res2_started.upto(a - 1))
                pool.tensor_tensor(res1[:, :, :], x_in[:, :, :], row[:, R_BO, None, :].broadcast_to([P, TILES, D]), ALU.add)\
                    .then_inc(res1_started.sem, 1)

            def left_chunk(f, c):
                pool.wait_ge(h_rounded.sem, h_rounded.upto(f, c))
                pool.wait_ge(h_used.sem, h_used.upto(f, c - 3))
                pool.tensor_tensor(h_lo[:, c % 3, :], gate[:, c % 2, :], h_hi[:, c % 3, :].bitcast(F32), ALU.subtract)\
                    .then_inc(h_left.sem, 1)

            def scale_probs(a, t):
                pool.wait_ge(s_share.sem, s_share.upto(a, t))
                pool.tensor_tensor(prob[:, t, :, :], prob[:, t, :, :],
                                   share[:, t, :, None].broadcast_to([P, HEADS, P]), ALU.mult).then_inc(p_scaled.sem, 1)

            def body(i, a, f, e, n):
                if f is not None:
                    for t in range(TILES):
                        rms(f, t, sq1, power1, scale1, mean1, rms1)
                    for t in range(TILES):
                        finish_x1(f, t)
                for c in range(FC):
                    if f is not None:
                        left_chunk(f, c)
                    if a is not None:
                        if c == 4:
                            scale_probs(a, 0)
                        if c == 8:
                            scale_probs(a, 1)
                    if e is not None and c == 6:
                        last_norm(e)
                    if f is not None and c == 7:
                        add_gamma(f)
                    if f is not None and c == 9:
                        start_res2(f)
                    if a is not None and c == FC - 1:
                        start_res1(a)
                if f is not None:
                    for t in range(TILES):
                        rms(f, t, sq2, power2, scale2, mean2, rms2)

            pipeline(pool, body)


MATS = 3
LATER, EARLIER, ITSELF = range(3)
G_ROWS = LAYERS * MATS * KC
R_BIAS, R_LNW, R_LNB = 0, LAYERS * MATS, LAYERS * MATS + 1
M_FAR, M_SIDES = 0, 1


def graph_block(nc, mid, adj, weights, cols, rows, ident, masks, out):
    ctx = ExitStack()
    with ctx:
        def sb(name, shape, dt=F32):
            return ctx.enter_context(nc.sbuf_tensor("g_" + name, shape, dt))

        def sem(name):
            return ctx.enter_context(nc.semaphore("g_" + name))

        def sig(name, per_step=1, unit=1):
            return Signal(sem(name), per_step, unit)

        def both(make, name, *args):
            return [make(f"{name}{l}", *args) for l in range(LAYERS)]

        w_hi = sb("w_hi", [P, G_ROWS, D], F32R)
        w_lo = sb("w_lo", [P, G_ROWS, D], F32R)
        col = sb("col", [P, 2 * KC])
        row = sb("row", [P, LAYERS * MATS + 2, D])
        idn = sb("idn", [P, P])
        mask = sb("mask", [P, 4, P])
        half_power = sb("half_power", [P, TILES])
        stage = sb("stage", [P, 2, 2 * D])
        m_in = sb("m_in", [P, TILES, D])
        m_res = sb("m_res", [P, TILES, D])
        near = both(sb, "near", [P, TILES, P])
        hT = both(sb, "hT", [P, KC, STEP])
        hT_hi = both(sb, "hT_hi", [P, KC, STEP], F32R)
        hT_lo = both(sb, "hT_lo", [P, KC, STEP], F32R)
        att = both(sb, "att", [P, TILES, P])
        peak = both(sb, "peak", [P, TILES])
        shift = both(sb, "shift", [P, TILES])
        total = both(sb, "total", [P, TILES])
        kept = both(sb, "kept", [P, TILES])
        share = both(sb, "share", [P, TILES])
        own = both(sb, "own", [P, TILES])
        sided = both(sb, "sided", [P, TILES, 3, P])
        sT_hi = both(sb, "sT_hi", [P, TILES, 2, P], F32R)
        sT_lo = both(sb, "sT_lo", [P, TILES, 2, P], F32R)
        side = both(sb, "side", [P, 2, D])
        side_hi = both(sb, "side_hi", [P, TILES, 2, D], F32R)
        side_lo = both(sb, "side_lo", [P, TILES, 2, D], F32R)
        acc = both(sb, "acc", [P, TILES, D])
        stats = both(sb, "stats", [P, TILES, 6])
        moments = both(sb, "moments", [P, TILES, 2])
        rstd = both(sb, "rstd", [P, TILES])
        offset = both(sb, "offset", [P, TILES])
        normed = both(sb, "normed", [P, TILES, D])
        last = sb("last", [P, TILES, D])
        result = sb("result", [P, TILES, D])
        f_stats = sb("f_stats", [P, TILES, 6])
        f_moments = sb("f_moments", [P, TILES, 2])
        f_rstd = sb("f_rstd", [P, TILES])
        f_offset = sb("f_offset", [P, TILES])

        banks = ctx.enter_context(nc.psum_tensor("g_banks", [P, 8, 512], F32))
        wide = banks[:, 0:2, :].rearrange("p b n -> p (b n)")[:, 0:KC * STEP]

        piece_in = [sem("piece_in0"), sem("piece_in1")]
        const_in, consts = sem("const_in"), sem("consts")
        w_rounded, w_left = sem("w_rounded"), sem("w_left")
        passed_dve, passed_pool = sem("passed_dve"), sem("passed_pool")
        m_loaded = sig("m_loaded", 1, 16)
        res_loaded = sig("res_loaded", 1, 16)
        near_loaded = both(sig, "near_loaded", 2, 16)
        stored = sig("stored", 1, 16)
        hT_ready = both(sig, "hT_ready")
        hT_copied = both(sig, "hT_copied")
        hT_rounded = both(sig, "hT_rounded")
        hT_left = both(sig, "hT_left")
        u_ready = both(sig, "u_ready")
        u_masked = both(sig, "u_masked")
        u_peak = both(sig, "u_peak")
        u_shift = both(sig, "u_shift")
        u_exp = both(sig, "u_exp")
        u_kept = both(sig, "u_kept")
        u_sum = both(sig, "u_sum")
        u_share = both(sig, "u_share")
        u_sided = both(sig, "u_sided")
        sT_ready = both(sig, "sT_ready")
        sT_rounded = both(sig, "sT_rounded")
        sT_left = both(sig, "sT_left")
        prod_ready = both(sig, "prod_ready", 6)
        prod_biased = both(sig, "prod_biased", 6)
        side_rounded = both(sig, "side_rounded", 4)
        side_left = both(sig, "side_left", 4)
        c_ready = both(sig, "c_ready", TILES)
        c_summed = both(sig, "c_summed", TILES)
        c_stats = both(sig, "c_stats", TILES)
        c_moments = both(sig, "c_moments", TILES)
        c_var = both(sig, "c_var")
        c_rstd = both(sig, "c_rstd")
        c_prod = both(sig, "c_prod")
        c_offset = both(sig, "c_offset")
        c_normed = both(sig, "c_normed")
        g_scaled = sig("g_scaled")
        g_shifted = sig("g_shifted")
        g_summed = sig("g_summed")
        g_stats = sig("g_stats")
        g_moments = sig("g_moments")
        g_var, g_rstd, g_prod, g_offset = sig("g_var"), sig("g_rstd"), sig("g_prod"), sig("g_offset")
        g_normed = sig("g_normed")

        block = ctx.enter_context(nc.Block())

        @block.sync
        def _(sp):
            for s in (m_loaded, res_loaded, *near_loaded, stored):
                sp.sem_inc(s.sem, s.whole)
            sp.dma_start(col[:, :], cols).then_inc(const_in, 16)
            sp.dma_start(idn[:, :], ident).then_inc(const_in, 16)
            sp.dma_start(mask[:, :, :], masks).then_inc(const_in, 16)
            sp.dma_start(row[:, :, :], rows).then_inc(const_in, 16)
            in_steps = mid.rearrange("(s t p) d -> s p t d", t=TILES, p=P)
            out_steps = out.rearrange("(s t p) d -> s p t d", t=TILES, p=P)
            adj_steps = adj.rearrange("(s t p) n -> s p t n", t=TILES, p=P)

            def load_m(n):
                sp.wait_ge(hT_ready[0].sem, hT_ready[0].upto(n - 1))
                sp.wait_ge(consts, 3)
                sp.dma_start(m_in[:, :, :], in_steps[n]).then_inc(m_loaded.sem, 16)

            def load_near(l, j):
                sp.wait_ge(u_kept[l].sem, u_kept[l].upto(j - 1))
                sp.wait_ge(consts, 3)
                for g in range(2):
                    lanes = slice(g * NODES, (g + 1) * NODES)
                    sp.dma_start(near[l][lanes, :, lanes], adj_steps[j, lanes]).then_inc(near_loaded[l].sem, 16)

            for n in range(G_ROWS // 2):
                if n >= 2:
                    sp.wait_ge(w_left, n - 1)
                sp.dma_start(stage[:, n % 2, :], weights[:, n * 2 * D:(n + 1) * 2 * D]).then_inc(piece_in[n % 2], 16)
            load_m(0)
            load_near(0, 0)

            def body(i, a, f, e, n):
                if n is not None:
                    load_near(0, n)
                if a is not None:
                    load_near(1, a)
                if n is not None:
                    load_m(n)
                if e is not None:
                    sp.wait_ge(g_summed.sem, g_summed.upto(e - 1))
                    sp.wait_ge(consts, 3)
                    sp.dma_start(m_res[:, :, :], in_steps[e]).then_inc(res_loaded.sem, 16)
                    sp.wait_ge(g_normed.sem, g_normed.upto(e))
                    sp.wait_ge(consts, 3)
                    sp.dma_start(out_steps[e], result[:, :, :]).then_inc(stored.sem, 16)

            pipeline(sp, body)
            sp.wait_ge(stored.sem, stored.upto(STEPS - 1))

        @block.tensor
        def _(pe):
            for pair in (hT_ready, u_ready, sT_ready, prod_ready, c_ready):
                for s in pair:
                    pe.sem_inc(s.sem, s.whole)
            pe.wait_ge(w_left, G_ROWS // 2)
            pe.wait_ge(const_in, 64)

            def transpose_input(l, j):
                if l == 0:
                    pe.wait_ge(m_loaded.sem, m_loaded.upto(j))
                    pe.wait_ge(hT_rounded[1].sem, hT_rounded[1].upto(j - 2))
                else:
                    pe.wait_ge(c_normed[0].sem, c_normed[0].upto(j))
                    pe.wait_ge(hT_rounded[0].sem, hT_rounded[0].upto(latest(j)))
                src = m_in if l == 0 else normed[0]
                for t in range(TILES):
                    for k in range(KC):
                        mm = pe.transpose(wide[:, k * STEP + t * P:k * STEP + (t + 1) * P], src[:, t, k * P:(k + 1) * P],
                                          idn[:, :])
                mm.then_inc(hT_ready[l].sem, 1)

            def scores(l, j):
                pe.wait_ge(hT_copied[l].sem, hT_copied[l].upto(j))
                if l == 0:
                    pe.wait_ge(sT_left[1].sem, sT_left[1].upto(j - 2))
                else:
                    pe.wait_ge(u_masked[0].sem, u_masked[0].upto(latest(j)))
                for t in range(TILES):
                    tokens = slice(t * P, (t + 1) * P)
                    for k in range(KC):
                        mm = pe.matmul(banks[:, 2, tokens], hT[l][:, k, tokens], hT[l][:, k, tokens],
                                       start=(k == 0), stop=(k == KC - 1))
                mm.then_inc(u_ready[l].sem, 1)

            def products(l, j, first, end):
                pe.wait_ge(hT_left[l].sem, hT_left[l].upto(j))
                for n in range(first, end):
                    t, m = n // MATS, n % MATS
                    if n >= 3:
                        pe.wait_ge(prod_biased[l].sem, prod_biased[l].upto(j, n - 3))
                    elif l == 0:
                        pe.wait_ge(prod_biased[1].sem, prod_biased[1].upto(j - 2, n + 3))
                    else:
                        pe.wait_ge(prod_biased[0].sem, prod_biased[0].upto(latest(j), n + 3))
                    r = (l * MATS + m) * KC
                    terms = [(k, x, w) for k in range(KC) for x, w in
                             ((hT_hi[l], w_hi), (hT_hi[l], w_lo), (hT_lo[l], w_hi))]
                    for q, (k, x, w) in enumerate(terms):
                        mm = pe.matmul(banks[:, 3 + n % 3, 0:D], x[:, k, t * P:(t + 1) * P], w[:, r + k, :],
                                       start=(q == 0), stop=(q == len(terms) - 1))
                    mm.then_inc(prod_ready[l].sem, 1)

            def transpose_sides(l, j):
                pe.wait_ge(u_sided[l].sem, u_sided[l].upto(j))
                if l == 0:
                    pe.wait_ge(u_masked[1].sem, u_masked[1].upto(j - 1))
                    pe.wait_ge(u_masked[0].sem, u_masked[0].upto(j))
                else:
                    pe.wait_ge(sT_left[0].sem, sT_left[0].upto(latest(j)))
                for t in range(TILES):
                    for side_ in range(2):
                        n = 2 * t + side_
                        mm = pe.transpose(banks[:, 2, n * P:(n + 1) * P], sided[l][:, t, side_, :], idn[:, :])
                mm.then_inc(sT_ready[l].sem, 1)

            def contexts(l, j):
                pe.wait_ge(sT_left[l].sem, sT_left[l].upto(j))
                for t in range(TILES):
                    pe.wait_ge(side_left[l].sem, side_left[l].upto(j, 2 * t + 1))
                    pe.wait_ge(c_summed[1 - l].sem, c_summed[1 - l].upto(j - 2 if l == 0 else latest(j), t))
                    terms = [(s, x, y) for s in range(2) for x, y in
                             ((sT_hi[l], side_hi[l]), (sT_hi[l], side_lo[l]), (sT_lo[l], side_hi[l]))]
                    for q, (s, x, y) in enumerate(terms):
                        mm = pe.matmul(banks[:, 6 + t, 0:D], x[:, t, s, :], y[:, t, s, :],
                                       start=(q == 0), stop=(q == len(terms) - 1))
                    mm.then_inc(c_ready[l].sem, 1)

            transpose_input(0, 0)

            def body(i, a, f, e, n):
                if a is not None:
                    scores(0, a)
                    products(0, a, 0, 4)
                if f is not None:
                    transpose_input(1, f)
                if a is not None:
                    products(0, a, 4, 6)
                if f is not None:
                    scores(1, f)
                    products(1, f, 0, 3)
                if a is not None:
                    transpose_sides(0, a)
                if f is not None:
                    products(1, f, 3, 6)
                    transpose_sides(1, f)
                if a is not None:
                    contexts(0, a)
                if n is not None:
                    transpose_input(0, n)
                if f is not None:
                    contexts(1, f)

            pipeline(pe, body)

        @block.scalar
        def _(act):
            for pair in (hT_copied, hT_rounded, u_exp, sT_rounded, side_rounded, c_normed):
                for s in pair:
                    act.sem_inc(s.sem, s.whole)
            act.sem_inc(g_normed.sem, g_normed.whole)
            act.wait_ge(const_in, 64)

            def copy_input(l, j):
                act.wait_ge(hT_ready[l].sem, hT_ready[l].upto(j))
                act.wait_ge(hT_left[l].sem, hT_left[l].upto(j - 1))
                act.wait_ge(u_ready[l].sem, u_ready[l].upto(j - 1))
                act.wait_ge(prod_ready[l].sem, prod_ready[l].upto(j - 1))
                for dst, done in ((hT[l], hT_copied[l]), (hT_hi[l], hT_rounded[l])):
                    if l == 0:
                        ins = act.activation(dst[:, :, :].rearrange("p k n -> p (k n)"), wide, ACT.Copy)
                    else:
                        for k in range(KC):
                            ins = act.activation(dst[:, k, :], wide[:, k * STEP:(k + 1) * STEP], ACT.Relu,
                                                 bias=col[:, KC + k:KC + k + 1], scale=col[:, k:k + 1])
                    ins.then_inc(done.sem, 1)

            def exps(l, j):
                act.wait_ge(u_shift[l].sem, u_shift[l].upto(j))
                for t in range(TILES):
                    ins = act.activation(att[l][:, t, :], att[l][:, t, :], ACT.Exp, bias=shift[l][:, t:t + 1],
                                         accum_out=total[l][:, t:t + 1])
                ins.then_inc(u_exp[l].sem, 1)

            def round_sides(l, j):
                act.wait_ge(sT_ready[l].sem, sT_ready[l].upto(j))
                act.wait_ge(c_ready[l].sem, c_ready[l].upto(j - 1))
                act.activation(sT_hi[l][:, :, :, :].rearrange("p t s n -> p (t s n)"), banks[:, 2, :], ACT.Copy)\
                    .then_inc(sT_rounded[l].sem, 1)

            def round_products(l, j, first, end):
                for n in range(first, end):
                    t, s = n // 2, n % 2
                    act.wait_ge(prod_biased[l].sem, prod_biased[l].upto(j, t * MATS + s))
                    act.wait_ge(c_ready[l].sem, c_ready[l].upto(j - 1, t))
                    act.activation(side_hi[l][:, t, s, :], side[l][:, s, :], ACT.Copy).then_inc(side_rounded[l].sem, 1)

            def norm_context(l, j):
                act.wait_ge(c_offset[l].sem, c_offset[l].upto(j))
                if l == 0:
                    act.wait_ge(hT_ready[1].sem, hT_ready[1].upto(j - 1))
                else:
                    act.wait_ge(g_summed.sem, g_summed.upto(j - 1))
                for t in range(TILES):
                    ins = act.activation(normed[l][:, t, :], acc[l][:, t, :], ACT.Identity,
                                         bias=offset[l][:, t:t + 1], scale=rstd[l][:, t:t + 1])
                ins.then_inc(c_normed[l].sem, 1)

            def last_norm(e):
                act.wait_ge(g_offset.sem, g_offset.upto(e))
                act.wait_ge(stored.sem, stored.upto(e - 1))
                for t in range(TILES):
                    ins = act.activation(result[:, t, :], last[:, t, :], ACT.Identity,
                                         bias=f_offset[:, t:t + 1], scale=f_rstd[:, t:t + 1])
                ins.then_inc(g_normed.sem, 1)

            copy_input(0, 0)

            def body(i, a, f, e, n):
                if a is not None:
                    exps(0, a)
                    round_products(0, a, 0, 2)
                if f is not None:
                    copy_input(1, f)
                if a is not None:
                    round_products(0, a, 2, 4)
                if f is not None:
                    exps(1, f)
                    round_products(1, f, 0, 2)
                if a is not None:
                    round_sides(0, a)
                if f is not None:
                    round_products(1, f, 2, 4)
                    round_sides(1, f)
                if n is not None:
                    copy_input(0, n)
                if a is not None:
                    norm_context(0, a)
                if f is not None:
                    norm_context(1, f)
                if e is not None:
                    last_norm(e)

            pipeline(act, body)

        @block.vector
        def _(dve):
            for pair in (u_masked, u_peak, u_shift, u_kept, u_sum, u_share, u_sided, sT_left,
                         prod_biased, c_summed, c_stats, c_moments):
                for s in pair:
                    dve.sem_inc(s.sem, s.whole)
            for s in (g_summed, g_stats, g_moments):
                dve.sem_inc(s.sem, s.whole)
            dve.memset(near[0][:, :, :], 0.0).then_inc(consts, 1)
            dve.memset(near[1][:, :, :], 0.0).then_inc(consts, 1)
            dve.memset(half_power[:, :], -0.5).then_inc(consts, 1)
            for n in range(G_ROWS // 2):
                src = stage[:, n % 2, :].rearrange("p (r d) -> p r d", d=D)
                piece = slice(2 * n, 2 * n + 2)
                dve.wait_ge(piece_in[n % 2], 16 * (n // 2 + 1))
                dve.tensor_copy(w_hi[:, piece, :], src).then_inc(w_rounded, 1)
                dve.wait_ge(w_rounded, n + 1)
                dve.tensor_tensor(w_lo[:, piece, :], src, w_hi[:, piece, :].bitcast(F32), ALU.subtract)\
                    .then_inc(w_left, 1)
            dve.wait_ge(const_in, 64)

            def mask_scores(l, j):
                dve.wait_ge(u_ready[l].sem, u_ready[l].upto(j))
                dve.scalar_tensor_tensor(out=att[l][:, :, :], in0=banks[:, 2, 0:STEP].rearrange("p (t n) -> p t n", t=TILES),
                                         scalar=U_SCALE, in1=mask[:, M_FAR:M_FAR + 1, :].broadcast_to([P, TILES, P]),
                                         op0=ALU.mult, op1=ALU.add).then_inc(u_masked[l].sem, 1)
                dve.wait_ge(u_masked[l].sem, u_masked[l].upto(j))
                dve.tensor_reduce(peak[l][:, :], att[l][:, :, :], AX_X, ALU.max).then_inc(u_peak[l].sem, 1)
                dve.wait_ge(u_peak[l].sem, u_peak[l].upto(j))
                dve.tensor_scalar(shift[l][:, :], peak[l][:, :], -1.0, None, ALU.mult).then_inc(u_shift[l].sem, 1)

            def attention(l, j):
                dve.wait_ge(u_exp[l].sem, u_exp[l].upto(j))
                dve.wait_ge(near_loaded[l].sem, near_loaded[l].upto(j))
                for t in range(TILES):
                    ins = dve.scalar_tensor_tensor(out=att[l][:, t, :], in0=att[l][:, t, :], scalar=1.0,
                                                   in1=near[l][:, t, :], op0=ALU.mult, op1=ALU.mult,
                                                   accum_out=kept[l][:, t:t + 1])
                ins.then_inc(u_kept[l].sem, 1)
                dve.wait_ge(u_kept[l].sem, u_kept[l].upto(j))
                dve.scalar_tensor_tensor(out=total[l][:, :], in0=total[l][:, :], scalar=1e-10, in1=kept[l][:, :],
                                         op0=ALU.mult, op1=ALU.add).then_inc(u_sum[l].sem, 1)
                dve.wait_ge(u_sum[l].sem, u_sum[l].upto(j))
                dve.reciprocal(share[l][:, :], total[l][:, :]).then_inc(u_share[l].sem, 1)
                dve.wait_ge(u_share[l].sem, u_share[l].upto(j))
                dve.wait_ge(sT_ready[l].sem, sT_ready[l].upto(j - 1))
                for t in range(TILES):
                    for s in range(MATS):
                        ins = dve.scalar_tensor_tensor(out=sided[l][:, t, s, :], in0=att[l][:, t, :],
                                                       scalar=share[l][:, t:t + 1], in1=mask[:, M_SIDES + s, :],
                                                       op0=ALU.mult, op1=ALU.mult,
                                                       accum_out=own[l][:, t:t + 1] if s == ITSELF else None)
                ins.then_inc(u_sided[l].sem, 1)

            def add_biases(l, j, first, end):
                for n in range(first, end):
                    t, m = n // MATS, n % MATS
                    dve.wait_ge(prod_ready[l].sem, prod_ready[l].upto(j, n))
                    if m == ITSELF:
                        dve.wait_ge(c_normed[l].sem, c_normed[l].upto(j - 1))
                        dst = acc[l][:, t, :]
                    else:
                        dve.wait_ge(side_left[l].sem, side_left[l].upto(j if t else j - 1, m if t else 2 + m))
                        dve.wait_ge(side_rounded[l].sem, side_rounded[l].upto(j if t else j - 1, m if t else 2 + m))
                        dst = side[l][:, m, :]
                    dve.tensor_tensor(dst, banks[:, 3 + n % 3, 0:D], row[:, R_BIAS + l * MATS + m, :], ALU.add)\
                        .then_inc(prod_biased[l].sem, 1)

            def left_sides(l, j):
                dve.wait_ge(sT_rounded[l].sem, sT_rounded[l].upto(j))
                dve.wait_ge(c_ready[l].sem, c_ready[l].upto(j - 1))
                dve.tensor_tensor(sT_lo[l][:, :, :, :].rearrange("p t s n -> p (t s n)"), banks[:, 2, :],
                                  sT_hi[l][:, :, :, :].rearrange("p t s n -> p (t s n)").bitcast(F32), ALU.subtract)\
                    .then_inc(sT_left[l].sem, 1)

            def sum_context(l, j):
                for t in range(TILES):
                    dve.wait_ge(c_ready[l].sem, c_ready[l].upto(j, t))
                    dve.wait_ge(prod_biased[l].sem, prod_biased[l].upto(j))
                    dve.wait_ge(u_sided[l].sem, u_sided[l].upto(j))
                    dve.scalar_tensor_tensor(out=acc[l][:, t, :], in0=acc[l][:, t, :], scalar=own[l][:, t:t + 1],
                                             in1=banks[:, 6 + t, 0:D], op0=ALU.mult, op1=ALU.add)\
                        .then_inc(c_summed[l].sem, 1)

            def context_moments(l, j):
                for t in range(TILES):
                    dve.wait_ge(c_summed[l].sem, c_summed[l].upto(j, t))
                    dve.bn_stats(stats[l][:, t, :], acc[l][:, t, :]).then_inc(c_stats[l].sem, 1)
                for t in range(TILES):
                    dve.wait_ge(c_stats[l].sem, c_stats[l].upto(j, t))
                    dve.sem_inc(passed_dve, 1)
                    dve.bn_aggr(moments[l][:, t, :], stats[l][:, t, :]).then_inc(c_moments[l].sem, 1)

            def last_sum(e):
                dve.wait_ge(g_shifted.sem, g_shifted.upto(e))
                dve.wait_ge(res_loaded.sem, res_loaded.upto(e))
                dve.wait_ge(g_normed.sem, g_normed.upto(e - 1))
                dve.scalar_tensor_tensor(out=last[:, :, :], in0=normed[1][:, :, :], scalar=0.0, in1=m_res[:, :, :],
                                         op0=ALU.max, op1=ALU.add).then_inc(g_summed.sem, 1)
                dve.wait_ge(g_summed.sem, g_summed.upto(e))
                for t in range(TILES):
                    ins = dve.bn_stats(f_stats[:, t, :], last[:, t, :])
                ins.then_inc(g_stats.sem, 1)
                dve.wait_ge(g_stats.sem, g_stats.upto(e))
                dve.sem_inc(passed_dve, 1)
                for t in range(TILES):
                    ins = dve.bn_aggr(f_moments[:, t, :], f_stats[:, t, :])
                ins.then_inc(g_moments.sem, 1)

            def body(i, a, f, e, n):
                if a is not None:
                    mask_scores(0, a)
                    add_biases(0, a, 0, 2)
                    attention(0, a)
                    add_biases(0, a, 2, 4)
                if a is not None:
                    add_biases(0, a, 4, 6)
                if f is not None:
                    mask_scores(1, f)
                    add_biases(1, f, 0, 2)
                    attention(1, f)
                    add_biases(1, f, 2, 4)
                if a is not None:
                    left_sides(0, a)
                if f is not None:
                    add_biases(1, f, 4, 6)
                    left_sides(1, f)
                if a is not None:
                    sum_context(0, a)
                if a is not None:
                    context_moments(0, a)
                if e is not None:
                    last_sum(e)
                if f is not None:
                    sum_context(1, f)
                    context_moments(1, f)

            pipeline(dve, body)

        @block.gpsimd
        def _(pool):
            for pair in (hT_left, side_left, c_var, c_rstd, c_prod, c_offset):
                for s in pair:
                    pool.sem_inc(s.sem, s.whole)
            for s in (g_scaled, g_shifted, g_var, g_rstd, g_prod, g_offset):
                pool.sem_inc(s.sem, s.whole)
            pool.wait_ge(const_in, 64)
            pool.wait_ge(consts, 3)

            def left_input(l, j):
                pool.wait_ge(hT_rounded[l].sem, hT_rounded[l].upto(j))
                pool.wait_ge(prod_ready[l].sem, prod_ready[l].upto(j - 1))
                pool.tensor_tensor(hT_lo[l][:, :, :], hT[l][:, :, :], hT_hi[l][:, :, :].bitcast(F32), ALU.subtract)\
                    .then_inc(hT_left[l].sem, 1)

            def left_products(l, j, first, end):
                for n in range(first, end):
                    t, s = n // 2, n % 2
                    pool.wait_ge(side_rounded[l].sem, side_rounded[l].upto(j, n))
                    pool.wait_ge(c_ready[l].sem, c_ready[l].upto(j - 1, t))
                    pool.tensor_tensor(side_lo[l][:, t, s, :], side[l][:, s, :], side_hi[l][:, t, s, :].bitcast(F32),
                                       ALU.subtract).then_inc(side_left[l].sem, 1)

            def norm_terms(j, ready, mom, eps, rstd_, offset_, used, var, root, prod, done):
                pool.wait_ge(ready.sem, ready.upto(j))
                pool.wait_ge(used.sem, used.upto(j - 1))
                pool.sem_inc(passed_pool, 1)
                pool.tensor_scalar(rstd_[:, :], mom[:, :, 1], 1.0, eps, ALU.mult, ALU.add).then_inc(var.sem, 1)
                pool.wait_ge(var.sem, var.upto(j))
                pool.tensor_tensor(rstd_[:, :], rstd_[:, :], half_power[:, :], ALU.pow).then_inc(root.sem, 1)
                pool.wait_ge(root.sem, root.upto(j))
                pool.tensor_tensor(offset_[:, :], mom[:, :, 0], rstd_[:, :], ALU.mult).then_inc(prod.sem, 1)
                pool.wait_ge(prod.sem, prod.upto(j))
                pool.sem_inc(passed_pool, 1)
                pool.tensor_scalar(offset_[:, :], offset_[:, :], -1.0, None, ALU.mult).then_inc(done.sem, 1)

            def norm_layer(l, j):
                norm_terms(j, c_moments[l], moments[l], CTX_EPS, rstd[l], offset[l], c_normed[l],
                           c_var[l], c_rstd[l], c_prod[l], c_offset[l])

            def affine(e):
                pool.wait_ge(c_normed[1].sem, c_normed[1].upto(e))
                pool.tensor_tensor(normed[1][:, :, :], normed[1][:, :, :],
                                   row[:, R_LNW, None, :].broadcast_to([P, TILES, D]), ALU.mult).then_inc(g_scaled.sem, 1)
                pool.wait_ge(g_scaled.sem, g_scaled.upto(e))
                pool.tensor_tensor(normed[1][:, :, :], normed[1][:, :, :],
                                   row[:, R_LNB, None, :].broadcast_to([P, TILES, D]), ALU.add).then_inc(g_shifted.sem, 1)

            left_input(0, 0)

            def body(i, a, f, e, n):
                if a is not None:
                    left_products(0, a, 0, 2)
                if f is not None:
                    left_input(1, f)
                if a is not None:
                    left_products(0, a, 2, 4)
                if e is not None:
                    affine(e)
                if f is not None:
                    left_products(1, f, 0, 4)
                if n is not None:
                    left_input(0, n)
                if a is not None:
                    norm_layer(0, a)
                if f is not None:
                    norm_layer(1, f)
                if e is not None:
                    norm_terms(e, g_moments, f_moments, NORM_EPS, f_rstd, f_offset, g_normed, g_var, g_rstd, g_prod, g_offset)

            pipeline(pool, body)


def build(nc, a, out):
    mid = nc.dram_tensor("mid", (TOKENS, D), F32, kind="Internal").ap()
    attention_block(nc, a["x"], a["xT"], a["adj"], a["weights0"], a["cols0"], a["rows0"], a["ident"], mid)
    graph_block(nc, mid, a["adj"], a["weights1"], a["cols1"], a["rows1"], a["ident"], a["masks"], out)


def lay_out(inputs):
    v = {k: np.asarray(a) for k, a in inputs.items()}

    def chunks(w):
        return w.reshape(-1, P, w.shape[1]).transpose(1, 0, 2).reshape(P, -1)

    def columns(b):
        return b.reshape(-1, P).T

    x = v["x"].reshape(TOKENS, D)
    l0 = {k[7:]: a for k, a in v.items() if k.startswith("L0_gnn_")}
    l1 = {k[7:]: a for k, a in v.items() if k.startswith("L1_gnn_")}
    feature = [c * P + np.arange(P) for _, c in PIECES]
    piece_mask = np.stack([(f // DH == h) for (h, _), f in zip(PIECES, feature)], 1).astype(np.float32)
    node = np.arange(P)
    graph = node // NODES
    same = graph[:, None] == graph[None, :]
    masks = np.stack([np.where(same, 0.0, FAR), same & (node[None, :] > node[:, None]),
                      same & (node[None, :] < node[:, None]), node[None, :] == node[:, None]], 1).astype(np.float32)
    mats = [l1[w][l].T for l in range(LAYERS) for w in ("Wl", "Wr", "Ws")]
    out = {
        "x": x,
        "xT": x.T,
        "adj": v["adj"].reshape(TOKENS, NODES),
        "weights0": np.concatenate([chunks(l0["wo"][CTX_FEATURE.ravel()] if w == "wo" else l0[w])
                                    for w in ("wq", "wk", "wv", "wo", "w1", "w2")], 1),
        "cols0": np.concatenate([piece_mask, np.stack([l0["bq"][f] for f in feature], 1)]
                                + [columns(l0["bk"]), l0["bv"][CTX_FEATURE].T, columns(l0["b1"])], 1),
        "rows0": np.broadcast_to(np.stack([l0[b] for b in ("bo", "alpha1", "gamma1", "b2", "alpha2", "gamma2")]),
                                 (P, 6, D)),
        "weights1": np.concatenate([chunks(w) for w in mats], 1),
        "cols1": np.concatenate([columns(l1["ln_w"][0]), columns(l1["ln_b"][0])], 1),
        "rows1": np.broadcast_to(np.stack([l1[b][l] for l in range(LAYERS) for b in ("bl", "br", "bs")]
                                          + [l1["ln_w"][1], l1["ln_b"][1]]), (P, 8, D)),
        "ident": np.eye(P, dtype=np.float32),
        "masks": masks,
    }
    return {k: np.ascontiguousarray(a) for k, a in out.items()}


def kernel(**inputs):
    import concourse.bacc as bacc
    from concourse.bass_utils import run_bass_kernel_spmd

    arrays = lay_out(inputs)
    nc = bacc.Bacc("TRN2", target_bir_lowering=False, num_devices=1)
    aps = {k: nc.dram_tensor(f"in_{k}", a.shape, F32, kind="ExternalInput").ap() for k, a in arrays.items()}
    out = nc.dram_tensor("out_0", (TOKENS, D), F32, kind="ExternalOutput").ap()
    build(nc, aps, out)
    r = run_bass_kernel_spmd(nc, [{f"in_{k}": a for k, a in arrays.items()}], core_ids=[0])
    return r.results[0]["out_0"].reshape(GRAPHS, NODES, D)
```

```python
from contextlib import ExitStack

import numpy as np

import concourse.bass as bass
from concourse import mybir

F32 = mybir.dt.float32
F32R = mybir.dt.float32r
ALU = mybir.AluOpType
ACT = mybir.ActivationFunctionType
AX_X = mybir.AxisListType.X

P = 128
GRAPHS, NODES, D = 128, 64, 384
TOKENS = GRAPHS * NODES
TILES = 2
STEP = TILES * P
STEPS = TOKENS // STEP
KC = D // P
HEADS = 8
DH = D // HEADS
FF = 1536
FC = FF // P
DEPTH = 4
LAG = 3
LAYERS = 2
MATS = 3
G_ROWS = LAYERS * MATS * KC
G_PIECES = G_ROWS // 2
L0_PIECES = (MATS * KC + 1) // 2
QK_SCALE = float(DH) ** -0.5
U_SCALE = float(D) ** -0.5
RMS_EPS = 1e-6
NORM_EPS = 1e-5
CTX_EPS = 1e-12
FAR = -3.0e38

PIECES = [(h, c) for c in range(KC) for h in range(HEADS) if h * DH < (c + 1) * P and (h + 1) * DH > c * P]
NPIECE = len(PIECES)
HALF = P // 2
GAP = HALF - DH
CTX_FEATURE = np.array([[(2 * k + s) * DH + r if r < DH else (HEADS - 2 + s) * DH + GAP * k + r - DH
                         for s in range(2) for r in range(HALF)] for k in range(KC)])

WQ, WK, WV, WO, W1, W2 = 0, KC, 2 * KC, 3 * KC, 4 * KC, 4 * KC + KC * FF // D
WROWS = W2 + FC
C_MASK, C_BQ, C_BK, C_BV, C_B1 = 0, NPIECE, 2 * NPIECE, 2 * NPIECE + KC, 2 * NPIECE + 2 * KC
C_COLS = C_B1 + FC
R_BO, R_A1, R_G1, R_B2, R_A2, R_G2 = range(6)
SCRATCH = max(NPIECE * STEP + KC * STEP + TILES * D + (TILES + 1) * HEADS * P, G_PIECES * 2 * D)


PIECES_FIRST, PIECES_LATE = W1 // 2, FC


class Signal:

    def __init__(self, sem, per_step=1, unit=1):
        self.sem, self.per_step, self.unit, self.whole = sem, per_step, unit, per_step * unit

    def upto(self, step, k=None):
        k = self.per_step - 1 if k is None else k
        value = (step * self.per_step + (self.per_step + k + 1)) * self.unit
        return max(value, 1) if isinstance(value, int) else value


def latest(j):
    return min(j + 1, STEPS - 1) if isinstance(j, int) else j + 1


def pipeline(eng, body):
    body(0, 0, None, None, 1)
    body(1, 1, 0, None, 2)
    with eng.Fori(2, STEPS - 1) as i:
        body(i, i, i - 1, i - 2, i + 1)
    body(STEPS - 1, STEPS - 1, STEPS - 2, STEPS - 3, None)
    body(STEPS, None, STEPS - 1, STEPS - 2, None)
    body(STEPS + 1, None, None, STEPS - 1, None)


def attention_block(nc, x, xT, adj, weights, cols, rows, ident, mid, scratch, next_weights, next_in):
    ctx = ExitStack()
    with ctx:
        def sb(name, shape, dt=F32):
            return ctx.enter_context(nc.sbuf_tensor(name, shape, dt))

        def sig(name, per_step=1, unit=1):
            return Signal(ctx.enter_context(nc.semaphore("a_" + name)), per_step, unit)

        def sem(name):
            return ctx.enter_context(nc.semaphore("a_" + name))

        w_hi = sb("w_hi", [P, WROWS, D], F32R)
        w_lo = sb("w_lo", [P, WROWS, D], F32R)
        w1_hi = w_hi[:, W1:W2, :].rearrange("p (k c) d -> p k (c d)", k=KC)
        w1_lo = w_lo[:, W1:W2, :].rearrange("p (k c) d -> p k (c d)", k=KC)
        col = sb("col", [P, C_COLS])
        row = sb("row", [P, 6, D])
        idn = sb("idn", [P, P])
        half_power = sb("half_power", [P, TILES])
        x_in = sb("x_in", [P, TILES, D])
        xT_in = sb("xT_in", [P, KC, STEP])
        xT_hi = sb("xT_hi", [P, KC, STEP], F32R)
        xT_lo = sb("xT_lo", [P, KC, STEP], F32R)
        bias = sb("bias", [P, TILES, P])
        at = np.cumsum([0, NPIECE * STEP, KC * STEP, TILES * D, TILES * HEADS * P, HEADS * P]).tolist()
        q_piece = scratch[:, at[0]:at[1]].rearrange("p (j n) -> p j n", n=STEP)
        kT = scratch[:, at[1]:at[2]].rearrange("p (k n) -> p k n", n=STEP)
        v = scratch[:, at[2]:at[3]].rearrange("p (t d) -> p t d", d=D)
        prob = scratch[:, at[3]:at[4]].rearrange("p (t h n) -> p t h n", t=TILES, n=P)
        probT = scratch[:, at[4]:at[5]].rearrange("p (h n) -> p h n", n=P)
        peak = sb("peak", [P, TILES, HEADS])
        shift = sb("shift", [P, TILES, HEADS])
        total = sb("total", [P, TILES, HEADS])
        share = sb("share", [P, TILES, HEADS])
        headsT = sb("headsT", [P, HEADS // 2, STEP])
        ctxT_hi = sb("ctxT_hi", [P, KC, STEP], F32R)
        ctxT_lo = sb("ctxT_lo", [P, KC, STEP], F32R)
        res1 = sb("res1", [P, TILES, D])
        res2 = sb("res2", [P, TILES, D])
        x_gamma = sb("x_gamma", [P, TILES, D])
        squares = sb("squares", [P, TILES, D])
        power1 = sb("power1", [P, TILES])
        scale1 = sb("scale1", [P, TILES])
        power2 = sb("power2", [P, TILES])
        scale2 = sb("scale2", [P, TILES])
        stats = sb("stats", [P, TILES, 6])
        moments = sb("moments", [P, TILES, 2])
        rstd = sb("rstd", [P, TILES])
        offset = sb("offset", [P, TILES])
        normed = sb("normed", [P, TILES, D])
        x1T_hi = sb("x1T_hi", [P, KC, STEP], F32R)
        x1T_lo = sb("x1T_lo", [P, KC, STEP], F32R)
        tanh = sb("tanh", [P, 2, STEP])
        half = sb("half", [P, 2, STEP])
        gate = sb("gate", [P, 2, STEP])
        h_hi = sb("h_hi", [P, DEPTH, STEP], F32R)
        h_lo = sb("h_lo", [P, DEPTH, STEP], F32R)

        work = ctx.enter_context(nc.psum_tensor("work", [P, 4, 512], F32))
        hidden = ctx.enter_context(nc.psum_tensor("hidden", [P, 2, 512], F32))
        y = ctx.enter_context(nc.psum_tensor("y", [P, 2, 512], F32))

        def low(k, n):
            return work[:, k:k + (n + 511) // 512, :].rearrange("p b n -> p (b n)")[:, 0:n]

        flat = q_piece[:, :, :].rearrange("p j n -> p (j n)")
        first_stage = [prob[:, t, :, :].rearrange("p h n -> p (h n)")[:, 0:2 * D] for t in range(TILES)]
        first_stage += [flat[:, n * 2 * D:(n + 1) * 2 * D] for n in range(3)]
        first_stage += [kT[:, :, :].rearrange("p k n -> p (k n)")]
        late_stage = [b[:, :, :].rearrange("p t d -> p (t d)") for b in (res2, x_gamma, normed, squares)]
        late = len(late_stage)

        def piece(n):
            landed = first_stage[n] if n < PIECES_FIRST else late_stage[(n - PIECES_FIRST) % late]
            return landed.rearrange("p (r d) -> p r d", d=D)


        first_in = [sem(f"first_in{n}") for n in range(PIECES_FIRST)]
        late_in = [sem(f"late_in{n}") for n in range(late)]
        const_in, row_in, consts = sem("const_in"), sem("row_in"), sem("consts")
        w_rounded, w_left = sem("w_rounded"), sem("w_left")
        passed_dve, passed_pool = sem("passed_dve"), sem("passed_pool")
        x_loaded = sig("x_loaded", 1, 16)
        xT_loaded = sig("xT_loaded", 1, 16)
        bias_loaded = sig("bias_loaded", 2, 16)
        ctx_moved = sig("ctx_moved", 2 * KC, 16)
        stored = sig("stored", 1, 16)
        xT_rounded = sig("xT_rounded")
        xT_left = sig("xT_left")
        q_ready = sig("q_ready", KC)
        k_ready = sig("k_ready", KC)
        v_ready = sig("v_ready", TILES)
        q_act = sig("q_act", 2)
        q_dve = sig("q_dve", 1)
        k_copied = sig("k_copied", KC)
        v_copied = sig("v_copied", TILES)
        s_ready = sig("s_ready", 2 * TILES)
        s_biased = sig("s_biased", 2 * TILES)
        s_peak = sig("s_peak", 2 * TILES)
        s_shift = sig("s_shift", TILES)
        s_exp = sig("s_exp", TILES)
        s_share = sig("s_share", TILES)
        p_scaled = sig("p_scaled", TILES)
        pT_ready = sig("pT_ready", TILES)
        pT_act = sig("pT_act", TILES)
        pT_dve = sig("pT_dve", TILES)
        c_ready = sig("c_ready", TILES)
        c_act = sig("c_act", TILES)
        c_dve = sig("c_dve", TILES)
        c_rounded = sig("c_rounded", KC)
        c_left = sig("c_left", KC)
        o_ready = sig("o_ready", TILES)
        o_added = sig("o_added", TILES)
        sq1 = sig("sq1", TILES)
        rms1 = sig("rms1", 2 * TILES)
        x1_scaled = sig("x1_scaled", TILES)
        x1_done = sig("x1_done", TILES)
        x1T_ready = sig("x1T_ready")
        x1T_rounded = sig("x1T_rounded")
        x1T_left = sig("x1T_left")
        h_ready = sig("h_ready", FC)
        h_tanh = sig("h_tanh", FC)
        h_half = sig("h_half", FC)
        h_gate = sig("h_gate", FC)
        h_rounded = sig("h_rounded", FC)
        h_left = sig("h_left", FC)
        y_added = sig("y_added", TILES)
        h_used = sig("h_used", FC)
        sq2 = sig("sq2", TILES)
        rms2 = sig("rms2", 2 * TILES)
        z_scaled = sig("z_scaled", TILES)
        z_done = sig("z_done", TILES)
        z_stats = sig("z_stats", TILES)
        z_moments = sig("z_moments", TILES)
        z_offset = sig("z_offset", 4)
        z_normed = sig("z_normed", TILES)
        res2_started = sig("res2_started")
        x_gamma_done = sig("x_gamma_done")
        res1_started = sig("res1_started")

        block = ctx.enter_context(nc.Block())

        @block.sync
        def _(sp):
            for s in (x_loaded, xT_loaded, bias_loaded, ctx_moved, stored):
                sp.sem_inc(s.sem, s.whole)
            sp.dma_start(col[:, :], cols).then_inc(const_in, 16)
            sp.dma_start(idn[:, :], ident).then_inc(const_in, 16)

            def load_xT(n):
                sp.wait_ge(xT_left.sem, xT_left.upto(n - 1))
                sp.wait_ge(consts, 2)
                sp.dma_start(xT_in[:, :, :], xT.rearrange("(k p) n -> p k n", p=P)[:, :, bass.ts(n, STEP)])\
                    .then_inc(xT_loaded.sem, 16)

            def load_bias(a):
                sp.wait_ge(s_biased.sem, s_biased.upto(a - 1))
                sp.wait_ge(consts, 2)
                for g in range(2):
                    lanes = slice(g * NODES, (g + 1) * NODES)
                    sp.dma_start(bias[lanes, :, lanes],
                                 adj.rearrange("(s t p) n -> s p t n", t=TILES, p=P)[a, lanes])\
                        .then_inc(bias_loaded.sem, 16)

            for n in range(PIECES_FIRST):
                sp.dma_start(piece(n), weights[:, n * 2 * D:(n + 1) * 2 * D]).then_inc(first_in[n], 16)
            sp.wait_ge(consts, 2)
            load_xT(0)

            def load_late(m):
                n = PIECES_FIRST + m
                if m >= late:
                    sp.wait_ge(w_left, n - late + 1)
                sp.dma_start(piece(n), weights[:, n * 2 * D:(n + 1) * 2 * D]).then_inc(late_in[m % late], 16)

            def body(i, a, f, e, n):
                if a is not None:
                    load_bias(a)
                if n is not None:
                    load_xT(n)
                if a is not None:
                    sp.wait_ge(x_gamma_done.sem, x_gamma_done.upto(a - 1))
                    sp.wait_ge(consts, 2)
                    sp.dma_start(x_in[:, :, :], x.rearrange("(s t p) d -> s p t d", t=TILES, p=P)[a])\
                        .then_inc(x_loaded.sem, 16)
                if a is None and f is not None:
                    for m in range(G_PIECES):
                        sp.dma_start(scratch[:, m * 2 * D:(m + 1) * 2 * D], next_weights[:, m * 2 * D:(m + 1) * 2 * D])\
                            .then_inc(next_in[m], 16)
                if f is None and a is not None:
                    for m in range(late):
                        load_late(m)
                    sp.dma_start(row[:, :, :], rows).then_inc(row_in, 16)
                    for m in range(late, PIECES_LATE):
                        load_late(m)
                if e is not None:
                    sp.wait_ge(z_normed.sem, z_normed.upto(e))
                    sp.wait_ge(consts, 2)
                    sp.dma_start(mid.rearrange("(s t p) d -> s p t d", t=TILES, p=P)[e], normed[:, :, :])\
                        .then_inc(stored.sem, 16)
                if a is not None:
                    sp.wait_ge(c_act.sem, c_act.upto(a))
                    sp.wait_ge(c_dve.sem, c_dve.upto(a))
                    for top in (0, HALF):
                        for k in range(KC):
                            sp.dma_start(headsT[top + DH:top + HALF, k, :],
                                         headsT[top + GAP * k:top + GAP * (k + 1), KC, :]).then_inc(ctx_moved.sem, 16)

            pipeline(sp, body)
            sp.wait_ge(stored.sem, stored.upto(STEPS - 1))

        @block.tensor
        def _(pe):
            for s in (q_ready, k_ready, v_ready, s_ready, pT_ready, c_ready, o_ready, x1T_ready,
                      h_ready, h_used):
                pe.sem_inc(s.sem, s.whole)
            pe.wait_ge(w_left, PIECES_FIRST)
            pe.wait_ge(const_in, 32)

            def product(out, left, right, ks):
                terms = [(k, u, w) for k in ks for u, w in ((0, 0), (0, 1), (1, 0))]
                for n, (k, u, w) in enumerate(terms):
                    mm = pe.matmul(out, left[u](k), right[w](k), start=(n == 0), stop=(n == len(terms) - 1))
                return mm

            def rows_of(w, r):
                return (lambda k: w_hi[:, r + k, :], lambda k: w_lo[:, r + k, :])

            def qk_chunk(a, w, m, bank):
                return product(low(bank, STEP),
                               (lambda k: w_hi[:, w + k, m * P:(m + 1) * P], lambda k: w_lo[:, w + k, m * P:(m + 1) * P]),
                               (lambda k: xT_hi[:, k, :], lambda k: xT_lo[:, k, :]), range(KC))

            def queries_keys(a):
                pe.wait_ge(xT_left.sem, xT_left.upto(a))
                pe.wait_ge(pT_act.sem, pT_act.upto(a - 1))
                pe.wait_ge(pT_dve.sem, pT_dve.upto(a - 1))
                for m in range(KC):
                    if m == 2:
                        pe.wait_ge(c_act.sem, c_act.upto(a - 1))
                        pe.wait_ge(c_dve.sem, c_dve.upto(a - 1))
                    qk_chunk(a, WQ, m, m).then_inc(q_ready.sem, 1)
                for m in range(KC):
                    if m:
                        prior = q_act if m == 1 else q_dve
                        pe.wait_ge(prior.sem, prior.upto(a, 0))
                    qk_chunk(a, WK, m, (3 + m) % 4).then_inc(k_ready.sem, 1)

            def transpose_x1(f, a):
                if a is not None:
                    pe.wait_ge(v_copied.sem, v_copied.upto(a))
                for t in range(TILES):
                    pe.wait_ge(x1_done.sem, x1_done.upto(f, t))
                    for k in range(KC):
                        mm = pe.transpose(low(0, KC * STEP)[:, k * STEP + t * P:k * STEP + (t + 1) * P],
                                          res1[:, t, k * P:(k + 1) * P], idn[:, :])
                mm.then_inc(x1T_ready.sem, 1)

            def token_major(out, left_hi, left_lo, t, w):
                return product(out, (lambda k: left_hi[:, k, t * P:(t + 1) * P], lambda k: left_lo[:, k, t * P:(t + 1) * P]),
                               rows_of(None, w), range(KC))

            def values(a, t):
                pe.wait_ge(k_copied.sem, k_copied.upto(a, t + 1))
                token_major(low(t, D), xT_hi, xT_lo, t, WV).then_inc(v_ready.sem, 1)

            def scores(a, f, t):
                if t == 0 and f is not None:
                    pe.wait_ge(o_added.sem, o_added.upto(f))
                elif t == 0:
                    pe.wait_ge(k_copied.sem, k_copied.upto(a, 0))
                pe.wait_ge(k_copied.sem, k_copied.upto(a))
                pe.wait_ge(q_act.sem, q_act.upto(a))
                pe.wait_ge(q_dve.sem, q_dve.upto(a))
                s = low(2, HEADS * P)
                for h in range(HEADS):
                    if t == 1 and h % 4 == 0:
                        pe.wait_ge(s_biased.sem, s_biased.upto(a, h // 4))
                    own = [j for j, (head, _) in enumerate(PIECES) if head == h]
                    for j in own:
                        mm = pe.matmul(s[:, h * P:(h + 1) * P], q_piece[:, j, t * P:(t + 1) * P],
                                       kT[:, PIECES[j][1], t * P:(t + 1) * P], start=(j == own[0]), stop=(j == own[-1]))
                    if h % 4 == 3:
                        mm.then_inc(s_ready.sem, 1)

            def transpose_probs(a, f, t):
                pe.wait_ge(p_scaled.sem, p_scaled.upto(a, t))
                if t == 1:
                    pe.wait_ge(pT_act.sem, pT_act.upto(a, 0))
                    pe.wait_ge(pT_dve.sem, pT_dve.upto(a, 0))
                elif f is not None:
                    pe.wait_ge(x1T_left.sem, x1T_left.upto(f))
                else:
                    pe.wait_ge(v_copied.sem, v_copied.upto(a))
                for h in range(HEADS):
                    mm = pe.transpose(low(0, HEADS * P)[:, h * P:(h + 1) * P], prob[:, t, h, :], idn[:, :])
                mm.then_inc(pT_ready.sem, 1)

            def contexts(a, t):
                pe.wait_ge(pT_act.sem, pT_act.upto(a, t))
                pe.wait_ge(pT_dve.sem, pT_dve.upto(a, t))
                pe.wait_ge(v_copied.sem, v_copied.upto(a, t))
                pe.wait_ge(s_biased.sem, s_biased.upto(a))
                for h in range(HEADS):
                    base = 64 * (h % 2)
                    mm = pe.matmul(work[base:base + DH, 2 + t, (h // 2) * P:(h // 2 + 1) * P],
                                   v[:, t, h * DH:(h + 1) * DH], probT[:, h, :], start=True, stop=True)
                mm.then_inc(c_ready.sem, 1)

            def hidden_chunk(f, c):
                if c == 0:
                    pe.wait_ge(w_left, PIECES_FIRST + PIECES_LATE)
                    pe.wait_ge(x1T_rounded.sem, x1T_rounded.upto(f))
                    pe.wait_ge(x1T_left.sem, x1T_left.upto(f))
                pe.wait_ge(h_half.sem, h_half.upto(f, c - 2))
                product(hidden[:, c % 2, 0:STEP],
                        (lambda k: w1_hi[:, k, c * P:(c + 1) * P], lambda k: w1_lo[:, k, c * P:(c + 1) * P]),
                        (lambda k: x1T_hi[:, k, :], lambda k: x1T_lo[:, k, :]), range(KC)).then_inc(h_ready.sem, 1)

            def down(f, c):
                pe.wait_ge(h_rounded.sem, h_rounded.upto(f, c))
                pe.wait_ge(h_left.sem, h_left.upto(f, c))
                if c == 0:
                    pe.wait_ge(y_added.sem, y_added.upto(f - 1))
                for t in range(TILES):
                    for n, (hh, ww) in enumerate(((h_hi, w_hi), (h_hi, w_lo), (h_lo, w_hi))):
                        mm = pe.matmul(y[:, t, 0:D], hh[:, c % DEPTH, t * P:(t + 1) * P], ww[:, W2 + c, :],
                                       start=(c == 0 and n == 0), stop=(c == FC - 1 and n == 2))
                mm.then_inc(h_used.sem, 1)

            def output(a, keys_too):
                pe.wait_ge(c_rounded.sem, c_rounded.upto(a))
                pe.wait_ge(c_left.sem, c_left.upto(a))
                if keys_too:
                    pe.wait_ge(q_act.sem, q_act.upto(a + 1))
                    pe.wait_ge(k_copied.sem, k_copied.upto(a + 1, 0))
                for t in range(TILES):
                    token_major(low(2 + t, D), ctxT_hi, ctxT_lo, t, WO).then_inc(o_ready.sem, 1)

            def body(i, a, f, e, n):
                if a is not None:
                    queries_keys(a)
                    values(a, 0)
                if f is not None:
                    output(f, a is not None)
                if a is not None:
                    values(a, 1)
                    scores(a, f, 0)
                if f is not None:
                    transpose_x1(f, a)
                if a is not None:
                    scores(a, f, 1)
                for c in range(FC):
                    if f is not None:
                        hidden_chunk(f, c)
                        if c >= LAG:
                            down(f, c - LAG)
                    if a is not None:
                        if c == 7:
                            transpose_probs(a, f, 0)
                        if c == 8:
                            contexts(a, 0)
                        if c == 11:
                            transpose_probs(a, f, 1)
                if f is not None:
                    down(f, FC - LAG)
                if a is not None:
                    contexts(a, 1)
                if f is not None:
                    for c in range(FC - LAG + 1, FC):
                        down(f, c)

            pipeline(pe, body)

        @block.scalar
        def _(act):
            for s in (xT_rounded, q_act, s_exp, pT_act, c_act, c_rounded, sq1, x1T_rounded, h_tanh,
                      h_rounded, sq2, z_normed):
                act.sem_inc(s.sem, s.whole)
            for n in range(PIECES_FIRST):
                act.wait_ge(first_in[n], 16)
                act.activation(w_hi[:, 2 * n:2 * n + 2, :], piece(n), ACT.Copy).then_inc(w_rounded, 1)
            act.wait_ge(const_in, 32)
            act.wait_ge(consts, 4)

            def round_late(m):
                n = PIECES_FIRST + m
                act.wait_ge(late_in[m % late], 16 * (m // late + 1))
                act.activation(w_hi[:, 2 * n:2 * n + 2, :], piece(n), ACT.Copy).then_inc(w_rounded, 1)

            def round_xT(n):
                act.wait_ge(xT_loaded.sem, xT_loaded.upto(n))
                act.wait_ge(v_ready.sem, v_ready.upto(n - 1))
                act.activation(xT_hi[:, :, :], xT_in[:, :, :], ACT.Copy).then_inc(xT_rounded.sem, 1)

            def query_pieces(a, m):
                act.wait_ge(q_ready.sem, q_ready.upto(a, m))
                if m == 0:
                    act.wait_ge(s_ready.sem, s_ready.upto(a - 1))
                own = [j for j, (_, c) in enumerate(PIECES) if c == m]
                for j in own:
                    ins = act.activation(q_piece[:, j, :], low(m, STEP), ACT.Identity,
                                         bias=col[:, C_BQ + j:C_BQ + j + 1], scale=col[:, C_MASK + j:C_MASK + j + 1])
                ins.then_inc(q_act.sem, 1)

            def exps(a, t, heads):
                if heads[0] == 0:
                    act.wait_ge(s_shift.sem, s_shift.upto(a, t))
                for h in heads:
                    ins = act.activation(prob[:, t, h, :], prob[:, t, h, :], ACT.Exp,
                                         bias=shift[:, t, h:h + 1], accum_out=total[:, t, h:h + 1])
                if heads[-1] == HEADS - 1:
                    ins.then_inc(s_exp.sem, 1)

            def copy_probT(a, t):
                act.wait_ge(pT_ready.sem, pT_ready.upto(a, t))
                act.wait_ge(c_ready.sem, c_ready.upto(a - 1 if t == 0 else a, 1 - t))
                act.activation(probT[:, 0:4, :], work[:, 0, :].rearrange("p (h n) -> p h n", n=P), ACT.Copy)\
                    .then_inc(pT_act.sem, 1)

            def copy_heads(a, t):
                act.wait_ge(c_ready.sem, c_ready.upto(a, t))
                act.wait_ge(c_rounded.sem, c_rounded.upto(a - 1))
                act.wait_ge(c_left.sem, c_left.upto(a - 1))
                act.activation(headsT[0:DH, :, t * P:(t + 1) * P],
                               work[0:DH, 2 + t, :].rearrange("p (h n) -> p h n", n=P), ACT.Copy).then_inc(c_act.sem, 1)

            def round_ctx(a):
                act.wait_ge(ctx_moved.sem, ctx_moved.upto(a))
                act.wait_ge(o_ready.sem, o_ready.upto(a - 1))
                for k in range(KC):
                    act.activation(ctxT_hi[:, k, :], headsT[:, k, :], ACT.Identity, bias=col[:, C_BV + k:C_BV + k + 1])\
                        .then_inc(c_rounded.sem, 1)

            def square_sums(added, t, f, buf, power, done, other, last):
                act.wait_ge(added.sem, added.upto(f, t))
                act.wait_ge(other.sem, other.upto(last, t))
                act.activation(squares[:, t, :], buf[:, t, :], ACT.Square, accum_out=power[:, t:t + 1])\
                    .then_inc(done.sem, 1)

            def round_x1T(f):
                act.wait_ge(x1T_ready.sem, x1T_ready.upto(f))
                act.wait_ge(h_ready.sem, h_ready.upto(f - 1))
                act.activation(x1T_hi[:, :, :].rearrange("p k n -> p (k n)"), low(0, KC * STEP), ACT.Copy)\
                    .then_inc(x1T_rounded.sem, 1)

            def tanh_chunk(f, c):
                act.wait_ge(h_half.sem, h_half.upto(f, c))
                act.wait_ge(h_gate.sem, h_gate.upto(f, c - 2))
                act.activation(tanh[:, c % 2, :], half[:, c % 2, :], ACT.Tanh).then_inc(h_tanh.sem, 1)

            def round_chunk(f, c):
                act.wait_ge(h_gate.sem, h_gate.upto(f, c))
                act.wait_ge(h_used.sem, h_used.upto(f, c - DEPTH))
                act.activation(h_hi[:, c % DEPTH, :], gate[:, c % 2, :], ACT.Copy).then_inc(h_rounded.sem, 1)

            def norm_out(e):
                act.wait_ge(z_offset.sem, z_offset.upto(e))
                act.wait_ge(stored.sem, stored.upto(e - 1))
                for t in range(TILES):
                    act.activation(normed[:, t, :], res2[:, t, :], ACT.Identity, bias=offset[:, t:t + 1],
                                   scale=rstd[:, t:t + 1]).then_inc(z_normed.sem, 1)

            round_xT(0)

            def body(i, a, f, e, n):
                if a is not None:
                    query_pieces(a, 0)
                    query_pieces(a, 2)
                if f is not None:
                    round_ctx(f)
                if f is not None:
                    for t in range(TILES):
                        square_sums(o_added, t, f, res1, power1, sq1, sq2, f - 1)
                    round_x1T(f)
                for c in range(FC):
                    if f is not None:
                        tanh_chunk(f, c)
                        if c:
                            round_chunk(f, c - 1)
                    elif a is not None:
                        round_late(c)
                    if a is not None:
                        if c < 8:
                            exps(a, c // 4, range(2 * (c % 4), 2 * (c % 4) + 2))
                        if c == 7:
                            copy_probT(a, 0)
                        if c == 8:
                            copy_heads(a, 0)
                        if c == 11:
                            copy_probT(a, 1)
                    if e is not None and c == 8:
                        norm_out(e)
                    if n is not None and c == 9:
                        round_xT(n)
                if f is not None:
                    round_chunk(f, FC - 1)
                if a is not None:
                    copy_heads(a, 1)
                if f is not None:
                    for t in range(TILES):
                        square_sums(y_added, t, f, res2, power2, sq2, sq1, f)

            pipeline(act, body)

        @block.vector
        def _(dve):
            for s in (xT_left, q_dve, k_copied, v_copied, s_biased, s_peak, s_shift, s_share, pT_dve,
                      c_dve, c_left, o_added, x1_scaled, x1T_left, h_half, h_gate, y_added, z_scaled,
                      z_done, z_stats, z_moments):
                dve.sem_inc(s.sem, s.whole)
            dve.memset(bias[:, :, :], FAR).then_inc(consts, 1)
            dve.memset(half_power[:, :], -0.5).then_inc(consts, 1)
            dve.wait_ge(const_in, 32)
            dve.tensor_tensor(col[:, C_BQ:C_BQ + NPIECE], col[:, C_BQ:C_BQ + NPIECE], col[:, C_MASK:C_MASK + NPIECE],
                              ALU.mult).then_inc(consts, 1)
            dve.tensor_scalar(col[:, C_B1:C_B1 + FC], col[:, C_B1:C_B1 + FC], 0.5, None, ALU.mult)\
                .then_inc(consts, 1)
            for n in range(PIECES_FIRST):
                dve.wait_ge(w_rounded, n + 1)
                dve.tensor_tensor(w_lo[:, 2 * n:2 * n + 2, :], piece(n), w_hi[:, 2 * n:2 * n + 2, :].bitcast(F32),
                                  ALU.subtract).then_inc(w_left, 1)
            dve.wait_ge(consts, 4)

            def left_late(m):
                n = PIECES_FIRST + m
                dve.wait_ge(w_rounded, n + 1)
                dve.tensor_tensor(w_lo[:, 2 * n:2 * n + 2, :], piece(n), w_hi[:, 2 * n:2 * n + 2, :].bitcast(F32),
                                  ALU.subtract).then_inc(w_left, 1)

            def left_xT(n):
                dve.wait_ge(xT_rounded.sem, xT_rounded.upto(n))
                dve.wait_ge(v_ready.sem, v_ready.upto(n - 1))
                dve.tensor_tensor(xT_lo[:, :, :], xT_in[:, :, :], xT_hi[:, :, :].bitcast(F32), ALU.subtract)\
                    .then_inc(xT_left.sem, 1)

            def query_pieces(a, m):
                dve.wait_ge(q_ready.sem, q_ready.upto(a, m))
                dve.wait_ge(s_ready.sem, s_ready.upto(a - 1))
                own = [j for j, (_, c) in enumerate(PIECES) if c == m]
                for j in own:
                    ins = dve.tensor_scalar(q_piece[:, j, :], low(m, STEP), col[:, C_MASK + j:C_MASK + j + 1],
                                            col[:, C_BQ + j:C_BQ + j + 1], ALU.mult, ALU.add)
                ins.then_inc(q_dve.sem, 1)

            def keys(a, m):
                dve.wait_ge(k_ready.sem, k_ready.upto(a, m))
                if m == 0:
                    dve.wait_ge(s_ready.sem, s_ready.upto(a - 1))
                dve.tensor_scalar(kT[:, m, :], low((3 + m) % 4, STEP), col[:, C_BK + m:C_BK + m + 1], None, ALU.add)\
                    .then_inc(k_copied.sem, 1)

            def copy_values(a, t):
                dve.wait_ge(v_ready.sem, v_ready.upto(a, t))
                dve.wait_ge(c_ready.sem, c_ready.upto(a - 1, t))
                dve.tensor_copy(v[:, t, :], low(t, D)).then_inc(v_copied.sem, 1)

            def bias_scores(a, t, g):
                dve.wait_ge(s_ready.sem, s_ready.upto(a, 2 * t + g))
                dve.wait_ge(bias_loaded.sem, bias_loaded.upto(a))
                dve.wait_ge(pT_ready.sem, pT_ready.upto(a - 1, t))
                heads = slice(4 * g, 4 * g + 4)
                dve.scalar_tensor_tensor(out=prob[:, t, heads, :],
                                         in0=work[:, 2 + g, :].rearrange("p (h n) -> p h n", n=P),
                                         scalar=QK_SCALE, in1=bias[:, t, None, :].broadcast_to([P, 4, P]),
                                         op0=ALU.mult, op1=ALU.add).then_inc(s_biased.sem, 1)

            def softmax_peak(a, t, g):
                dve.wait_ge(s_biased.sem, s_biased.upto(a, 2 * t + g))
                heads = slice(4 * g, 4 * g + 4)
                dve.tensor_reduce(peak[:, t, heads], prob[:, t, heads, :], AX_X, ALU.max).then_inc(s_peak.sem, 1)
                if g == 1:
                    dve.wait_ge(s_peak.sem, s_peak.upto(a, 2 * t + 1))
                    dve.tensor_scalar(shift[:, t, :], peak[:, t, :], -1.0, None, ALU.mult).then_inc(s_shift.sem, 1)

            def softmax_share(a, t):
                dve.wait_ge(s_exp.sem, s_exp.upto(a, t))
                dve.reciprocal(share[:, t, :], total[:, t, :]).then_inc(s_share.sem, 1)

            def copy_probT(a, t):
                dve.wait_ge(pT_ready.sem, pT_ready.upto(a, t))
                dve.wait_ge(c_ready.sem, c_ready.upto(a - 1 if t == 0 else a, 1 - t))
                dve.tensor_copy(probT[:, 4:8, :], work[:, 1, :].rearrange("p (h n) -> p h n", n=P))\
                    .then_inc(pT_dve.sem, 1)

            def copy_heads(a, t):
                dve.wait_ge(c_ready.sem, c_ready.upto(a, t))
                dve.wait_ge(c_left.sem, c_left.upto(a - 1))
                dve.tensor_copy(headsT[64:64 + DH, :, t * P:(t + 1) * P],
                                work[64:64 + DH, 2 + t, :].rearrange("p (h n) -> p h n", n=P)).then_inc(c_dve.sem, 1)

            def left_ctx(a):
                dve.wait_ge(o_ready.sem, o_ready.upto(a - 1))
                for k in range(KC):
                    dve.wait_ge(c_rounded.sem, c_rounded.upto(a, k))
                    dve.scalar_tensor_tensor(out=ctxT_lo[:, k, :], in0=headsT[:, k, :], scalar=col[:, C_BV + k:C_BV + k + 1],
                                             in1=ctxT_hi[:, k, :].bitcast(F32), op0=ALU.add, op1=ALU.subtract)\
                        .then_inc(c_left.sem, 1)

            def add_output(f, t):
                dve.wait_ge(o_ready.sem, o_ready.upto(f, t))
                dve.wait_ge(res1_started.sem, res1_started.upto(f))
                dve.tensor_tensor(res1[:, t, :], low(2 + t, D), res1[:, t, :], ALU.add).then_inc(o_added.sem, 1)

            def scale_x1(f, t):
                dve.wait_ge(rms1.sem, rms1.upto(f, 2 * t + 1))
                dve.scalar_tensor_tensor(out=res1[:, t, :], in0=res1[:, t, :], scalar=scale1[:, t:t + 1],
                                         in1=row[:, R_A1, :], op0=ALU.mult, op1=ALU.mult).then_inc(x1_scaled.sem, 1)

            def left_x1T(f):
                dve.wait_ge(x1T_rounded.sem, x1T_rounded.upto(f))
                dve.wait_ge(h_ready.sem, h_ready.upto(f - 1))
                dve.tensor_tensor(x1T_lo[:, :, :].rearrange("p k n -> p (k n)"), low(0, KC * STEP),
                                  x1T_hi[:, :, :].rearrange("p k n -> p (k n)").bitcast(F32), ALU.subtract)\
                    .then_inc(x1T_left.sem, 1)

            def half_chunk(f, c):
                dve.wait_ge(h_ready.sem, h_ready.upto(f, c))
                dve.wait_ge(h_gate.sem, h_gate.upto(f, c - 2))
                dve.tensor_scalar(half[:, c % 2, :], hidden[:, c % 2, 0:STEP], 0.5, col[:, C_B1 + c:C_B1 + c + 1],
                                  ALU.mult, ALU.add).then_inc(h_half.sem, 1)

            def gate_chunk(f, c):
                dve.wait_ge(h_tanh.sem, h_tanh.upto(f, c))
                dve.wait_ge(h_rounded.sem, h_rounded.upto(f, c - 2))
                dve.wait_ge(h_left.sem, h_left.upto(f, c - 2))
                dve.scalar_tensor_tensor(out=gate[:, c % 2, :], in0=tanh[:, c % 2, :], scalar=1.0,
                                         in1=half[:, c % 2, :], op0=ALU.add, op1=ALU.mult).then_inc(h_gate.sem, 1)

            def add_down(f, t):
                dve.wait_ge(h_used.sem, h_used.upto(f))
                dve.wait_ge(res2_started.sem, res2_started.upto(f))
                dve.tensor_tensor(res2[:, t, :], y[:, t, 0:D], res2[:, t, :], ALU.add).then_inc(y_added.sem, 1)

            def last_sum(e, t):
                dve.wait_ge(rms2.sem, rms2.upto(e, 2 * t + 1))
                dve.scalar_tensor_tensor(out=res2[:, t, :], in0=res2[:, t, :], scalar=scale2[:, t:t + 1],
                                         in1=row[:, R_A2, :], op0=ALU.mult, op1=ALU.mult).then_inc(z_scaled.sem, 1)
                dve.wait_ge(z_scaled.sem, z_scaled.upto(e, t))
                dve.wait_ge(x_gamma_done.sem, x_gamma_done.upto(e))
                dve.tensor_tensor(res2[:, t, :], res2[:, t, :], x_gamma[:, t, :], ALU.add).then_inc(z_done.sem, 1)
                dve.wait_ge(z_done.sem, z_done.upto(e, t))
                dve.bn_stats(stats[:, t, :], res2[:, t, :]).then_inc(z_stats.sem, 1)
                dve.wait_ge(z_stats.sem, z_stats.upto(e, t))
                dve.sem_inc(passed_dve, 1)
                dve.bn_aggr(moments[:, t, :], stats[:, t, :]).then_inc(z_moments.sem, 1)

            left_xT(0)

            def body(i, a, f, e, n):
                if a is not None:
                    query_pieces(a, 1)
                    keys(a, 0)
                    keys(a, 1)
                if f is not None:
                    left_ctx(f)
                if a is not None:
                    keys(a, 2)
                    copy_values(a, 0)
                if f is not None:
                    for t in range(TILES):
                        add_output(f, t)
                    scale_x1(f, 0)
                if a is not None:
                    copy_values(a, 1)
                if f is not None:
                    scale_x1(f, 1)
                if a is not None:
                    bias_scores(a, 0, 0)
                    bias_scores(a, 0, 1)
                if f is not None:
                    left_x1T(f)
                if a is not None:
                    softmax_peak(a, 0, 0)
                    softmax_peak(a, 0, 1)
                for c in range(FC):
                    if f is not None:
                        half_chunk(f, c)
                        if c:
                            gate_chunk(f, c - 1)
                    elif a is not None:
                        left_late(c)
                    if a is not None:
                        if c < 2:
                            bias_scores(a, 1, c)
                        elif c < 4:
                            softmax_peak(a, 1, c - 2)
                        if c == 4:
                            softmax_share(a, 0)
                        if c == 7:
                            copy_probT(a, 0)
                        if c == 8:
                            copy_heads(a, 0)
                        if c == 8:
                            softmax_share(a, 1)
                        if c == 11:
                            copy_probT(a, 1)
                    if e is not None and c in (3, 5):
                        last_sum(e, (c - 3) // 2)
                    if n is not None and c == 9:
                        left_xT(n)
                if f is not None:
                    gate_chunk(f, FC - 1)
                if a is not None:
                    copy_heads(a, 1)
                if f is not None:
                    for t in range(TILES):
                        add_down(f, t)

            pipeline(dve, body)

        @block.gpsimd
        def _(pool):
            for s in (p_scaled, rms1, x1_done, h_left, rms2, z_offset,
                      res2_started, x_gamma_done, res1_started):
                pool.sem_inc(s.sem, s.whole)
            pool.wait_ge(row_in, 16)
            pool.wait_ge(consts, 2)

            def rms(f, t, done, power, scale, ready):
                pool.wait_ge(done.sem, done.upto(f, t))
                pool.sem_inc(passed_pool, 1)
                pool.tensor_scalar(power[:, t:t + 1], power[:, t:t + 1], 1.0 / D, RMS_EPS, ALU.mult, ALU.add)\
                    .then_inc(ready.sem, 1)
                pool.wait_ge(ready.sem, ready.upto(f, 2 * t))
                pool.tensor_tensor(scale[:, t:t + 1], power[:, t:t + 1], half_power[:, 0:1], ALU.pow)\
                    .then_inc(ready.sem, 1)

            def finish_x1(f, t):
                pool.wait_ge(x1_scaled.sem, x1_scaled.upto(f, t))
                pool.tensor_tensor(res1[:, t, :], res1[:, t, :], row[:, R_G1, :], ALU.add).then_inc(x1_done.sem, 1)

            def last_norm(e):
                pool.wait_ge(z_moments.sem, z_moments.upto(e))
                pool.sem_inc(passed_pool, 1)
                pool.tensor_scalar(rstd[:, :], moments[:, :, 1], 1.0, NORM_EPS, ALU.mult, ALU.add)\
                    .then_inc(z_offset.sem, 1)
                pool.wait_ge(z_offset.sem, z_offset.upto(e, 0))
                pool.tensor_tensor(rstd[:, :], rstd[:, :], half_power[:, :], ALU.pow).then_inc(z_offset.sem, 1)
                pool.wait_ge(z_offset.sem, z_offset.upto(e, 1))
                pool.tensor_tensor(offset[:, :], moments[:, :, 0], rstd[:, :], ALU.mult).then_inc(z_offset.sem, 1)
                pool.wait_ge(z_offset.sem, z_offset.upto(e, 2))
                pool.sem_inc(passed_pool, 1)
                pool.tensor_scalar(offset[:, :], offset[:, :], -1.0, None, ALU.mult).then_inc(z_offset.sem, 1)

            def start_res2(f):
                pool.wait_ge(x1_done.sem, x1_done.upto(f))
                pool.wait_ge(z_normed.sem, z_normed.upto(f - 1))
                pool.tensor_tensor(res2[:, :, :], res1[:, :, :], row[:, R_B2, None, :].broadcast_to([P, TILES, D]), ALU.add)\
                    .then_inc(res2_started.sem, 1)

            def add_gamma(f):
                pool.wait_ge(x_loaded.sem, x_loaded.upto(f))
                pool.wait_ge(z_done.sem, z_done.upto(f - 1))
                pool.tensor_tensor(x_gamma[:, :, :], x_in[:, :, :], row[:, R_G2, None, :].broadcast_to([P, TILES, D]), ALU.add)\
                    .then_inc(x_gamma_done.sem, 1)

            def start_res1(a):
                pool.wait_ge(x_loaded.sem, x_loaded.upto(a))
                pool.wait_ge(x1T_ready.sem, x1T_ready.upto(a - 1))
                pool.wait_ge(res2_started.sem, res2_started.upto(a - 1))
                pool.tensor_tensor(res1[:, :, :], x_in[:, :, :], row[:, R_BO, None, :].broadcast_to([P, TILES, D]), ALU.add)\
                    .then_inc(res1_started.sem, 1)

            def left_chunk(f, c):
                pool.wait_ge(h_rounded.sem, h_rounded.upto(f, c))
                pool.wait_ge(h_used.sem, h_used.upto(f, c - DEPTH))
                pool.tensor_tensor(h_lo[:, c % DEPTH, :], gate[:, c % 2, :], h_hi[:, c % DEPTH, :].bitcast(F32), ALU.subtract)\
                    .then_inc(h_left.sem, 1)

            def scale_probs(a, t):
                pool.wait_ge(s_share.sem, s_share.upto(a, t))
                pool.tensor_tensor(prob[:, t, :, :], prob[:, t, :, :],
                                   share[:, t, :, None].broadcast_to([P, HEADS, P]), ALU.mult).then_inc(p_scaled.sem, 1)

            def body(i, a, f, e, n):
                if f is not None:
                    for t in range(TILES):
                        rms(f, t, sq1, power1, scale1, rms1)
                    for t in range(TILES):
                        finish_x1(f, t)
                for c in range(FC):
                    if f is not None:
                        left_chunk(f, c)
                    if a is not None:
                        if c == 4:
                            scale_probs(a, 0)
                        if c == 8:
                            scale_probs(a, 1)
                    if e is not None and c == 6:
                        last_norm(e)
                    if f is not None and c == 7:
                        add_gamma(f)
                    if f is not None and c == 9:
                        start_res2(f)
                    if a is not None and c == FC - 1:
                        start_res1(a)
                if f is not None:
                    for t in range(TILES):
                        rms(f, t, sq2, power2, scale2, rms2)

            pipeline(pool, body)


LATER, EARLIER, ITSELF = range(3)
R_BIAS, R_LNW, R_LNB = 0, LAYERS * MATS, LAYERS * MATS + 1
SIDES_BANK = (7, 2)
M_FAR, M_SIDES = 0, 1


def graph_block(nc, mid, adj, cols, rows, ident, masks, out, stage, piece_in):
    ctx = ExitStack()
    with ctx:
        def sb(name, shape, dt=F32):
            return ctx.enter_context(nc.sbuf_tensor("g_" + name, shape, dt))

        def sem(name):
            return ctx.enter_context(nc.semaphore("g_" + name))

        def sig(name, per_step=1, unit=1):
            return Signal(sem(name), per_step, unit)

        def both(make, name, *args):
            return [make(f"{name}{l}", *args) for l in range(LAYERS)]

        w_hi = sb("w_hi", [P, G_ROWS, D], F32R)
        w_lo = sb("w_lo", [P, G_ROWS, D], F32R)
        col = sb("col", [P, 2 * KC])
        row = sb("row", [P, LAYERS * MATS + 2, D])
        idn = sb("idn", [P, P])
        mask = sb("mask", [P, 4, P])
        half_power = sb("half_power", [P, TILES])
        m_in = sb("m_in", [P, TILES, D])
        m_res = sb("m_res", [P, TILES, D])
        near = both(sb, "near", [P, TILES, P])
        hT = both(sb, "hT", [P, KC, STEP])
        hT_hi = both(sb, "hT_hi", [P, KC, STEP], F32R)
        hT_lo = both(sb, "hT_lo", [P, KC, STEP], F32R)
        att = both(sb, "att", [P, TILES, P])
        peak = both(sb, "peak", [P, TILES])
        shift = both(sb, "shift", [P, TILES])
        total = both(sb, "total", [P, TILES])
        kept = both(sb, "kept", [P, TILES])
        share = both(sb, "share", [P, TILES])
        own = both(sb, "own", [P, TILES])
        sided = both(sb, "sided", [P, TILES, 3, P])
        sT_hi = both(sb, "sT_hi", [P, TILES, 2, P], F32R)
        sT_lo = both(sb, "sT_lo", [P, TILES, 2, P], F32R)
        side = both(sb, "side", [P, TILES, 2, D])
        side_hi = both(sb, "side_hi", [P, TILES, 2, D], F32R)
        side_lo = both(sb, "side_lo", [P, TILES, 2, D], F32R)
        acc = both(sb, "acc", [P, TILES, D])
        stats = both(sb, "stats", [P, TILES, 6])
        moments = both(sb, "moments", [P, TILES, 2])
        rstd = both(sb, "rstd", [P, TILES])
        offset = both(sb, "offset", [P, TILES])
        normed = both(sb, "normed", [P, TILES, D])
        last = sb("last", [P, TILES, D])
        result = sb("result", [P, TILES, D])
        f_stats = sb("f_stats", [P, TILES, 6])
        f_moments = sb("f_moments", [P, TILES, 2])
        f_rstd = sb("f_rstd", [P, TILES])
        f_offset = sb("f_offset", [P, TILES])

        banks = ctx.enter_context(nc.psum_tensor("g_banks", [P, 8, 512], F32))
        def piece(n):
            return stage[:, n * 2 * D:(n + 1) * 2 * D].rearrange("p (r d) -> p r d", d=D)

        wide = banks[:, 0:2, :].rearrange("p b n -> p (b n)")[:, 0:KC * STEP]

        const_in, row_in, consts = sem("const_in"), sem("row_in"), sem("consts")
        w_rounded, w_left = sem("w_rounded"), sem("w_left")
        passed_dve, passed_pool = sem("passed_dve"), sem("passed_pool")
        m_loaded = sig("m_loaded", 1, 16)
        res_loaded = sig("res_loaded", 1, 16)
        near_loaded = both(sig, "near_loaded", 2, 16)
        stored = sig("stored", 1, 16)
        hT_ready = both(sig, "hT_ready")
        hT_copied = both(sig, "hT_copied")
        hT_rounded = both(sig, "hT_rounded")
        hT_left = both(sig, "hT_left")
        u_ready = both(sig, "u_ready")
        u_masked = both(sig, "u_masked")
        u_peak = both(sig, "u_peak")
        u_shift = both(sig, "u_shift")
        u_exp = both(sig, "u_exp")
        u_kept = both(sig, "u_kept")
        u_sum = both(sig, "u_sum")
        u_share = both(sig, "u_share")
        u_sided = both(sig, "u_sided")
        sT_ready = both(sig, "sT_ready")
        sT_rounded = both(sig, "sT_rounded")
        sT_left = both(sig, "sT_left")
        prod_ready = both(sig, "prod_ready", 6)
        prod_biased = both(sig, "prod_biased", 6)
        side_rounded = both(sig, "side_rounded", 4)
        side_left = both(sig, "side_left", 4)
        c_ready = both(sig, "c_ready", TILES)
        c_summed = both(sig, "c_summed", TILES)
        c_stats = both(sig, "c_stats", TILES)
        c_moments = both(sig, "c_moments", TILES)
        c_offset = both(sig, "c_offset", 4)
        c_normed = both(sig, "c_normed")
        g_scaled = sig("g_scaled")
        g_shifted = sig("g_shifted")
        g_summed = sig("g_summed")
        g_stats = sig("g_stats")
        g_moments = sig("g_moments")
        g_offset = sig("g_offset", 4)
        g_normed = sig("g_normed")

        block = ctx.enter_context(nc.Block())

        @block.sync
        def _(sp):
            for s in (m_loaded, res_loaded, *near_loaded, stored):
                sp.sem_inc(s.sem, s.whole)
            sp.dma_start(col[:, :], cols).then_inc(const_in, 16)
            sp.dma_start(idn[:, :], ident).then_inc(const_in, 16)
            in_steps = mid.rearrange("(s t p) d -> s p t d", t=TILES, p=P)
            out_steps = out.rearrange("(s t p) d -> s p t d", t=TILES, p=P)
            adj_steps = adj.rearrange("(s t p) n -> s p t n", t=TILES, p=P)

            def load_m(n):
                sp.wait_ge(hT_ready[0].sem, hT_ready[0].upto(n - 1))
                sp.wait_ge(consts, 3)
                sp.dma_start(m_in[:, :, :], in_steps[n]).then_inc(m_loaded.sem, 16)

            def load_near(l, j):
                sp.wait_ge(u_kept[l].sem, u_kept[l].upto(j - 1))
                sp.wait_ge(consts, 3)
                for g in range(2):
                    lanes = slice(g * NODES, (g + 1) * NODES)
                    sp.dma_start(near[l][lanes, :, lanes], adj_steps[j, lanes]).then_inc(near_loaded[l].sem, 16)

            load_m(0)
            load_near(0, 0)
            sp.dma_start(mask[:, :, :], masks).then_inc(row_in, 16)
            sp.dma_start(row[:, :, :], rows).then_inc(row_in, 16)

            def body(i, a, f, e, n):
                if n is not None:
                    load_m(n)
                if a is not None:
                    load_near(1, a)
                if n is not None:
                    load_near(0, n)
                if e is not None:
                    sp.wait_ge(g_summed.sem, g_summed.upto(e - 1))
                    sp.wait_ge(consts, 3)
                    sp.dma_start(m_res[:, :, :], in_steps[e]).then_inc(res_loaded.sem, 16)
                    sp.wait_ge(g_normed.sem, g_normed.upto(e))
                    sp.wait_ge(consts, 3)
                    sp.dma_start(out_steps[e], result[:, :, :]).then_inc(stored.sem, 16)

            pipeline(sp, body)
            sp.wait_ge(stored.sem, stored.upto(STEPS - 1))

        @block.tensor
        def _(pe):
            for pair in (hT_ready, u_ready, sT_ready, prod_ready, c_ready):
                for s in pair:
                    pe.sem_inc(s.sem, s.whole)
            pe.wait_ge(const_in, 32)

            def transpose_input(l, j):
                if l == 0:
                    pe.wait_ge(m_loaded.sem, m_loaded.upto(j))
                    pe.wait_ge(hT_rounded[1].sem, hT_rounded[1].upto(j - 2))
                else:
                    pe.wait_ge(c_normed[0].sem, c_normed[0].upto(j))
                    pe.wait_ge(hT_rounded[0].sem, hT_rounded[0].upto(latest(j)))
                src = m_in if l == 0 else normed[0]
                for t in range(TILES):
                    for k in range(KC):
                        mm = pe.transpose(wide[:, k * STEP + t * P:k * STEP + (t + 1) * P], src[:, t, k * P:(k + 1) * P],
                                          idn[:, :])
                mm.then_inc(hT_ready[l].sem, 1)

            def scores(l, j):
                pe.wait_ge(hT_copied[l].sem, hT_copied[l].upto(j))
                if l == 0:
                    pe.wait_ge(sT_left[1].sem, sT_left[1].upto(j - 2))
                else:
                    pe.wait_ge(u_masked[0].sem, u_masked[0].upto(latest(j)))
                for t in range(TILES):
                    tokens = slice(t * P, (t + 1) * P)
                    for k in range(KC):
                        mm = pe.matmul(banks[:, 2, tokens], hT[l][:, k, tokens], hT[l][:, k, tokens],
                                       start=(k == 0), stop=(k == KC - 1))
                mm.then_inc(u_ready[l].sem, 1)

            def products(l, j, first, end):
                if first == 0:
                    pe.wait_ge(w_left, L0_PIECES if l == 0 else G_PIECES)
                pe.wait_ge(hT_left[l].sem, hT_left[l].upto(j))
                for n in range(first, end):
                    t, m = n // MATS, n % MATS
                    if n >= 3:
                        pe.wait_ge(prod_biased[l].sem, prod_biased[l].upto(j, n - 3))
                    elif l == 0:
                        pe.wait_ge(prod_biased[1].sem, prod_biased[1].upto(j - 2, n + 3))
                    else:
                        pe.wait_ge(prod_biased[0].sem, prod_biased[0].upto(latest(j), n + 3))
                    r = (l * MATS + m) * KC
                    terms = [(k, x, w) for k in range(KC) for x, w in
                             ((hT_hi[l], w_hi), (hT_hi[l], w_lo), (hT_lo[l], w_hi))]
                    for q, (k, x, w) in enumerate(terms):
                        mm = pe.matmul(banks[:, 3 + n % 3, 0:D], x[:, k, t * P:(t + 1) * P], w[:, r + k, :],
                                       start=(q == 0), stop=(q == len(terms) - 1))
                    mm.then_inc(prod_ready[l].sem, 1)

            def transpose_sides(l, j):
                pe.wait_ge(u_sided[l].sem, u_sided[l].upto(j))
                if l == 0:
                    pe.wait_ge(c_summed[1].sem, c_summed[1].upto(j - 2))
                for t in range(TILES):
                    for side_ in range(2):
                        n = 2 * t + side_
                        mm = pe.transpose(banks[:, SIDES_BANK[l], n * P:(n + 1) * P], sided[l][:, t, side_, :], idn[:, :])
                mm.then_inc(sT_ready[l].sem, 1)

            def contexts(l, j):
                pe.wait_ge(sT_left[l].sem, sT_left[l].upto(j))
                for t in range(TILES):
                    pe.wait_ge(side_left[l].sem, side_left[l].upto(j, 2 * t + 1))
                    pe.wait_ge(c_summed[1 - l].sem, c_summed[1 - l].upto(j - 2 if l == 0 else latest(j), t))
                    terms = [(s, x, y) for s in range(2) for x, y in
                             ((sT_hi[l], side_hi[l]), (sT_hi[l], side_lo[l]), (sT_lo[l], side_hi[l]))]
                    for q, (s, x, y) in enumerate(terms):
                        mm = pe.matmul(banks[:, 6 + t, 0:D], x[:, t, s, :], y[:, t, s, :],
                                       start=(q == 0), stop=(q == len(terms) - 1))
                    mm.then_inc(c_ready[l].sem, 1)

            transpose_input(0, 0)

            def body(i, a, f, e, n):
                if a is not None:
                    scores(0, a)
                    products(0, a, 0, 2)
                if f is not None:
                    transpose_input(1, f)
                if a is not None:
                    products(0, a, 2, 6)
                if f is not None:
                    scores(1, f)
                if a is not None:
                    transpose_sides(0, a)
                if f is not None:
                    products(1, f, 0, 6)
                if n is not None:
                    transpose_input(0, n)
                if f is not None:
                    transpose_sides(1, f)
                if a is not None:
                    contexts(0, a)
                if f is not None:
                    contexts(1, f)

            pipeline(pe, body)

        @block.scalar
        def _(act):
            for pair in (hT_copied, hT_rounded, u_exp, sT_rounded, side_rounded, c_normed):
                for s in pair:
                    act.sem_inc(s.sem, s.whole)
            act.sem_inc(g_normed.sem, g_normed.whole)
            act.wait_ge(const_in, 32)

            def copy_input(l, j):
                act.wait_ge(hT_ready[l].sem, hT_ready[l].upto(j))
                act.wait_ge(hT_left[l].sem, hT_left[l].upto(j - 1))
                act.wait_ge(u_ready[l].sem, u_ready[l].upto(j - 1))
                act.wait_ge(prod_ready[l].sem, prod_ready[l].upto(j - 1))
                for dst, done in ((hT[l], hT_copied[l]), (hT_hi[l], hT_rounded[l])):
                    if l == 0:
                        ins = act.activation(dst[:, :, :].rearrange("p k n -> p (k n)"), wide, ACT.Copy)
                    else:
                        for k in range(KC):
                            ins = act.activation(dst[:, k, :], wide[:, k * STEP:(k + 1) * STEP], ACT.Relu,
                                                 bias=col[:, KC + k:KC + k + 1], scale=col[:, k:k + 1])
                    ins.then_inc(done.sem, 1)

            def exps(l, j):
                act.wait_ge(u_shift[l].sem, u_shift[l].upto(j))
                for t in range(TILES):
                    ins = act.activation(att[l][:, t, :], att[l][:, t, :], ACT.Exp, bias=shift[l][:, t:t + 1],
                                         accum_out=total[l][:, t:t + 1])
                ins.then_inc(u_exp[l].sem, 1)

            def round_sides(l, j):
                act.wait_ge(sT_ready[l].sem, sT_ready[l].upto(j))
                act.wait_ge(c_ready[l].sem, c_ready[l].upto(j - 1))
                act.activation(sT_hi[l][:, :, :, :].rearrange("p t s n -> p (t s n)"), banks[:, SIDES_BANK[l], :], ACT.Copy)\
                    .then_inc(sT_rounded[l].sem, 1)

            def round_products(l, j, first, end):
                for n in range(first, end):
                    t, s = n // 2, n % 2
                    act.wait_ge(prod_biased[l].sem, prod_biased[l].upto(j, t * MATS + s))
                    act.wait_ge(c_ready[l].sem, c_ready[l].upto(j - 1, t))
                    act.activation(side_hi[l][:, t, s, :], side[l][:, t, s, :], ACT.Copy).then_inc(side_rounded[l].sem, 1)

            def norm_context(l, j):
                act.wait_ge(c_offset[l].sem, c_offset[l].upto(j))
                if l == 0:
                    act.wait_ge(hT_ready[1].sem, hT_ready[1].upto(j - 1))
                else:
                    act.wait_ge(g_summed.sem, g_summed.upto(j - 1))
                for t in range(TILES):
                    ins = act.activation(normed[l][:, t, :], acc[l][:, t, :], ACT.Identity,
                                         bias=offset[l][:, t:t + 1], scale=rstd[l][:, t:t + 1])
                ins.then_inc(c_normed[l].sem, 1)

            def last_norm(e):
                act.wait_ge(g_offset.sem, g_offset.upto(e))
                act.wait_ge(stored.sem, stored.upto(e - 1))
                for t in range(TILES):
                    ins = act.activation(result[:, t, :], last[:, t, :], ACT.Identity,
                                         bias=f_offset[:, t:t + 1], scale=f_rstd[:, t:t + 1])
                ins.then_inc(g_normed.sem, 1)

            def round_pieces(first, end):
                for n in range(first, end):
                    act.wait_ge(piece_in[n], 16)
                    act.activation(w_hi[:, 2 * n:2 * n + 2, :], piece(n), ACT.Copy).then_inc(w_rounded, 1)

            round_pieces(0, L0_PIECES)
            copy_input(0, 0)
            round_pieces(L0_PIECES, G_PIECES)

            def body(i, a, f, e, n):
                if a is not None:
                    exps(0, a)
                if f is not None:
                    copy_input(1, f)
                if e is not None:
                    norm_context(1, e)
                if a is not None:
                    round_products(0, a, 0, 4)
                if f is not None:
                    exps(1, f)
                    round_products(1, f, 0, 2)
                if a is not None:
                    round_sides(0, a)
                if f is not None:
                    round_products(1, f, 2, 4)
                    round_sides(1, f)
                if n is not None:
                    copy_input(0, n)
                if a is not None:
                    norm_context(0, a)
                if e is not None:
                    last_norm(e)

            pipeline(act, body)

        @block.vector
        def _(dve):
            for pair in (u_masked, u_peak, u_shift, u_kept, u_sum, u_share, u_sided, sT_left,
                         prod_biased, c_summed, c_stats, c_moments):
                for s in pair:
                    dve.sem_inc(s.sem, s.whole)
            for s in (g_summed, g_stats, g_moments):
                dve.sem_inc(s.sem, s.whole)
            dve.memset(near[0][:, :, :], 0.0).then_inc(consts, 1)
            dve.memset(near[1][:, :, :], 0.0).then_inc(consts, 1)
            dve.memset(half_power[:, :], -0.5).then_inc(consts, 1)
            for n in range(G_PIECES):
                rows_ = slice(2 * n, 2 * n + 2)
                dve.wait_ge(w_rounded, n + 1)
                dve.tensor_tensor(w_lo[:, rows_, :], piece(n),
                                  w_hi[:, rows_, :].bitcast(F32), ALU.subtract).then_inc(w_left, 1)
            dve.wait_ge(row_in, 32)

            def mask_scores(l, j):
                dve.wait_ge(u_ready[l].sem, u_ready[l].upto(j))
                dve.scalar_tensor_tensor(out=att[l][:, :, :], in0=banks[:, 2, 0:STEP].rearrange("p (t n) -> p t n", t=TILES),
                                         scalar=U_SCALE, in1=mask[:, M_FAR:M_FAR + 1, :].broadcast_to([P, TILES, P]),
                                         op0=ALU.mult, op1=ALU.add).then_inc(u_masked[l].sem, 1)
                dve.wait_ge(u_masked[l].sem, u_masked[l].upto(j))
                dve.tensor_reduce(peak[l][:, :], att[l][:, :, :], AX_X, ALU.max).then_inc(u_peak[l].sem, 1)
                dve.wait_ge(u_peak[l].sem, u_peak[l].upto(j))
                dve.tensor_scalar(shift[l][:, :], peak[l][:, :], -1.0, None, ALU.mult).then_inc(u_shift[l].sem, 1)

            def attention(l, j):
                dve.wait_ge(u_exp[l].sem, u_exp[l].upto(j))
                dve.wait_ge(near_loaded[l].sem, near_loaded[l].upto(j))
                for t in range(TILES):
                    ins = dve.scalar_tensor_tensor(out=att[l][:, t, :], in0=att[l][:, t, :], scalar=1.0,
                                                   in1=near[l][:, t, :], op0=ALU.mult, op1=ALU.mult,
                                                   accum_out=kept[l][:, t:t + 1])
                ins.then_inc(u_kept[l].sem, 1)
                dve.wait_ge(u_kept[l].sem, u_kept[l].upto(j))
                dve.scalar_tensor_tensor(out=total[l][:, :], in0=total[l][:, :], scalar=1e-10, in1=kept[l][:, :],
                                         op0=ALU.mult, op1=ALU.add).then_inc(u_sum[l].sem, 1)
                dve.wait_ge(u_sum[l].sem, u_sum[l].upto(j))
                dve.reciprocal(share[l][:, :], total[l][:, :]).then_inc(u_share[l].sem, 1)
                dve.wait_ge(u_share[l].sem, u_share[l].upto(j))
                dve.wait_ge(sT_ready[l].sem, sT_ready[l].upto(j - 1))
                for t in range(TILES):
                    for s in range(MATS):
                        ins = dve.scalar_tensor_tensor(out=sided[l][:, t, s, :], in0=att[l][:, t, :],
                                                       scalar=share[l][:, t:t + 1], in1=mask[:, M_SIDES + s, :],
                                                       op0=ALU.mult, op1=ALU.mult,
                                                       accum_out=own[l][:, t:t + 1] if s == ITSELF else None)
                ins.then_inc(u_sided[l].sem, 1)

            def add_biases(l, j, first, end):
                for n in range(first, end):
                    t, m = n // MATS, n % MATS
                    dve.wait_ge(prod_ready[l].sem, prod_ready[l].upto(j, n))
                    if m == ITSELF:
                        dve.wait_ge(c_normed[l].sem, c_normed[l].upto(j - 1))
                        dst = acc[l][:, t, :]
                    else:
                        dve.wait_ge(side_rounded[l].sem, side_rounded[l].upto(j - 1, 2 * t + m))
                        dve.wait_ge(side_left[l].sem, side_left[l].upto(j - 1, 2 * t + m))
                        dst = side[l][:, t, m, :]
                    dve.tensor_tensor(dst, banks[:, 3 + n % 3, 0:D], row[:, R_BIAS + l * MATS + m, :], ALU.add)\
                        .then_inc(prod_biased[l].sem, 1)

            def left_sides(l, j):
                dve.wait_ge(sT_rounded[l].sem, sT_rounded[l].upto(j))
                dve.wait_ge(c_ready[l].sem, c_ready[l].upto(j - 1))
                dve.tensor_tensor(sT_lo[l][:, :, :, :].rearrange("p t s n -> p (t s n)"), banks[:, SIDES_BANK[l], :],
                                  sT_hi[l][:, :, :, :].rearrange("p t s n -> p (t s n)").bitcast(F32), ALU.subtract)\
                    .then_inc(sT_left[l].sem, 1)

            def sum_context(l, j):
                for t in range(TILES):
                    dve.wait_ge(c_ready[l].sem, c_ready[l].upto(j, t))
                    dve.wait_ge(prod_biased[l].sem, prod_biased[l].upto(j))
                    dve.wait_ge(u_sided[l].sem, u_sided[l].upto(j))
                    dve.scalar_tensor_tensor(out=acc[l][:, t, :], in0=acc[l][:, t, :], scalar=own[l][:, t:t + 1],
                                             in1=banks[:, 6 + t, 0:D], op0=ALU.mult, op1=ALU.add)\
                        .then_inc(c_summed[l].sem, 1)

            def context_moments(l, j):
                for t in range(TILES):
                    dve.wait_ge(c_summed[l].sem, c_summed[l].upto(j, t))
                    dve.bn_stats(stats[l][:, t, :], acc[l][:, t, :]).then_inc(c_stats[l].sem, 1)
                for t in range(TILES):
                    dve.wait_ge(c_stats[l].sem, c_stats[l].upto(j, t))
                    dve.sem_inc(passed_dve, 1)
                    dve.bn_aggr(moments[l][:, t, :], stats[l][:, t, :]).then_inc(c_moments[l].sem, 1)

            def last_sum(e):
                dve.wait_ge(g_shifted.sem, g_shifted.upto(e))
                dve.wait_ge(res_loaded.sem, res_loaded.upto(e))
                dve.wait_ge(g_normed.sem, g_normed.upto(e - 1))
                dve.scalar_tensor_tensor(out=last[:, :, :], in0=normed[1][:, :, :], scalar=0.0, in1=m_res[:, :, :],
                                         op0=ALU.max, op1=ALU.add).then_inc(g_summed.sem, 1)
                dve.wait_ge(g_summed.sem, g_summed.upto(e))
                for t in range(TILES):
                    ins = dve.bn_stats(f_stats[:, t, :], last[:, t, :])
                ins.then_inc(g_stats.sem, 1)
                dve.wait_ge(g_stats.sem, g_stats.upto(e))
                dve.sem_inc(passed_dve, 1)
                for t in range(TILES):
                    ins = dve.bn_aggr(f_moments[:, t, :], f_stats[:, t, :])
                ins.then_inc(g_moments.sem, 1)

            def body(i, a, f, e, n):
                if a is not None:
                    mask_scores(0, a)
                    add_biases(0, a, 0, 1)
                if e is not None:
                    sum_context(1, e)
                    context_moments(1, e)
                if a is not None:
                    add_biases(0, a, 1, 3)
                    attention(0, a)
                    add_biases(0, a, 3, 6)
                if f is not None:
                    mask_scores(1, f)
                    add_biases(1, f, 0, 3)
                    attention(1, f)
                if a is not None:
                    left_sides(0, a)
                if f is not None:
                    add_biases(1, f, 3, 6)
                    left_sides(1, f)
                if a is not None:
                    sum_context(0, a)
                    context_moments(0, a)
                if e is not None:
                    last_sum(e)

            pipeline(dve, body)

        @block.gpsimd
        def _(pool):
            for pair in (hT_left, side_left, c_offset):
                for s in pair:
                    pool.sem_inc(s.sem, s.whole)
            for s in (g_scaled, g_shifted, g_offset):
                pool.sem_inc(s.sem, s.whole)
            pool.wait_ge(row_in, 32)
            pool.wait_ge(consts, 3)

            def left_input(l, j):
                pool.wait_ge(hT_rounded[l].sem, hT_rounded[l].upto(j))
                pool.wait_ge(prod_ready[l].sem, prod_ready[l].upto(j - 1))
                pool.tensor_tensor(hT_lo[l][:, :, :], hT[l][:, :, :], hT_hi[l][:, :, :].bitcast(F32), ALU.subtract)\
                    .then_inc(hT_left[l].sem, 1)

            def left_products(l, j, first, end):
                for n in range(first, end):
                    t, s = n // 2, n % 2
                    pool.wait_ge(side_rounded[l].sem, side_rounded[l].upto(j, n))
                    pool.wait_ge(c_ready[l].sem, c_ready[l].upto(j - 1, t))
                    pool.tensor_tensor(side_lo[l][:, t, s, :], side[l][:, t, s, :], side_hi[l][:, t, s, :].bitcast(F32),
                                       ALU.subtract).then_inc(side_left[l].sem, 1)

            def norm_terms(j, ready, mom, eps, rstd_, offset_, used, done):
                pool.wait_ge(ready.sem, ready.upto(j))
                pool.wait_ge(used.sem, used.upto(j - 1))
                pool.sem_inc(passed_pool, 1)
                pool.tensor_scalar(rstd_[:, :], mom[:, :, 1], 1.0, eps, ALU.mult, ALU.add).then_inc(done.sem, 1)
                pool.wait_ge(done.sem, done.upto(j, 0))
                pool.tensor_tensor(rstd_[:, :], rstd_[:, :], half_power[:, :], ALU.pow).then_inc(done.sem, 1)
                pool.wait_ge(done.sem, done.upto(j, 1))
                pool.tensor_tensor(offset_[:, :], mom[:, :, 0], rstd_[:, :], ALU.mult).then_inc(done.sem, 1)
                pool.wait_ge(done.sem, done.upto(j, 2))
                pool.sem_inc(passed_pool, 1)
                pool.tensor_scalar(offset_[:, :], offset_[:, :], -1.0, None, ALU.mult).then_inc(done.sem, 1)

            def norm_layer(l, j):
                norm_terms(j, c_moments[l], moments[l], CTX_EPS, rstd[l], offset[l], c_normed[l], c_offset[l])

            def affine(e):
                pool.wait_ge(c_normed[1].sem, c_normed[1].upto(e))
                pool.tensor_tensor(normed[1][:, :, :], normed[1][:, :, :],
                                   row[:, R_LNW, None, :].broadcast_to([P, TILES, D]), ALU.mult).then_inc(g_scaled.sem, 1)
                pool.wait_ge(g_scaled.sem, g_scaled.upto(e))
                pool.tensor_tensor(normed[1][:, :, :], normed[1][:, :, :],
                                   row[:, R_LNB, None, :].broadcast_to([P, TILES, D]), ALU.add).then_inc(g_shifted.sem, 1)

            left_input(0, 0)

            def body(i, a, f, e, n):
                if e is not None:
                    norm_layer(1, e)
                if f is not None:
                    left_input(1, f)
                if a is not None:
                    left_products(0, a, 0, 4)
                if e is not None:
                    affine(e)
                if f is not None:
                    left_products(1, f, 0, 4)
                if n is not None:
                    left_input(0, n)
                if a is not None:
                    norm_layer(0, a)
                if e is not None:
                    norm_terms(e, g_moments, f_moments, NORM_EPS, f_rstd, f_offset, g_normed, g_offset)

            pipeline(pool, body)


def build(nc, a, out):
    mid = nc.dram_tensor("mid", (TOKENS, D), F32, kind="Internal").ap()
    with ExitStack() as ctx:
        scratch = ctx.enter_context(nc.sbuf_tensor("scratch", [P, SCRATCH], F32))
        piece_in = [ctx.enter_context(nc.semaphore(f"piece_in{n}")) for n in range(G_PIECES)]
        attention_block(nc, a["x"], a["xT"], a["adj"], a["weights0"], a["cols0"], a["rows0"], a["ident"], mid,
                        scratch, a["weights1"], piece_in)
        graph_block(nc, mid, a["adj"], a["cols1"], a["rows1"], a["ident"], a["masks"], out, scratch, piece_in)


def lay_out(inputs):
    v = {k: np.asarray(a) for k, a in inputs.items()}

    def chunks(w):
        return w.reshape(-1, P, w.shape[1]).transpose(1, 0, 2).reshape(P, -1)

    def columns(b):
        return b.reshape(-1, P).T

    x = v["x"].reshape(TOKENS, D)
    l0 = {k[7:]: a for k, a in v.items() if k.startswith("L0_gnn_")}
    l1 = {k[7:]: a for k, a in v.items() if k.startswith("L1_gnn_")}
    feature = [c * P + np.arange(P) for _, c in PIECES]
    piece_mask = np.stack([(f // DH == h) for (h, _), f in zip(PIECES, feature)], 1).astype(np.float32)
    node = np.arange(P)
    graph = node // NODES
    same = graph[:, None] == graph[None, :]
    masks = np.stack([np.where(same, 0.0, FAR), same & (node[None, :] > node[:, None]),
                      same & (node[None, :] < node[:, None]), node[None, :] == node[:, None]], 1).astype(np.float32)
    mats = [l1[w][l].T for l in range(LAYERS) for w in ("Wl", "Wr", "Ws")]
    out = {
        "x": x,
        "xT": x.T,
        "adj": v["adj"].reshape(TOKENS, NODES),
        "weights0": np.concatenate([chunks(l0["wo"][CTX_FEATURE.ravel()] if w == "wo" else l0[w])
                                    for w in ("wq", "wk", "wv", "wo", "w1", "w2")], 1),
        "cols0": np.concatenate([piece_mask, np.stack([l0["bq"][f] for f in feature], 1)]
                                + [columns(l0["bk"]), l0["bv"][CTX_FEATURE].T, columns(l0["b1"])], 1),
        "rows0": np.broadcast_to(np.stack([l0[b] for b in ("bo", "alpha1", "gamma1", "b2", "alpha2", "gamma2")]),
                                 (P, 6, D)),
        "weights1": np.concatenate([chunks(w) for w in mats], 1),
        "cols1": np.concatenate([columns(l1["ln_w"][0]), columns(l1["ln_b"][0])], 1),
        "rows1": np.broadcast_to(np.stack([l1[b][l] for l in range(LAYERS) for b in ("bl", "br", "bs")]
                                          + [l1["ln_w"][1], l1["ln_b"][1]]), (P, 8, D)),
        "ident": np.eye(P, dtype=np.float32),
        "masks": masks,
    }
    return {k: np.ascontiguousarray(a) for k, a in out.items()}


def kernel(**inputs):
    import concourse.bacc as bacc
    from concourse.bass_utils import run_bass_kernel_spmd

    arrays = lay_out(inputs)
    nc = bacc.Bacc("TRN2", target_bir_lowering=False, num_devices=1)
    aps = {k: nc.dram_tensor(f"in_{k}", a.shape, F32, kind="ExternalInput").ap() for k, a in arrays.items()}
    out = nc.dram_tensor("out_0", (TOKENS, D), F32, kind="ExternalOutput").ap()
    build(nc, aps, out)
    r = run_bass_kernel_spmd(nc, [{f"in_{k}": a for k, a in arrays.items()}], core_ids=[0])
    return r.results[0]["out_0"].reshape(GRAPHS, NODES, D)
```
